# Optimizing a Trainium2 kernel written in Bass

```python
import numpy as np
import jax
import jax.numpy as jnp

def _softmax(x, axis=-1):
    return jax.nn.softmax(x, axis=axis)

def _gelu(x):
    return jax.nn.gelu(x, approximate=True)

def _silu(x):
    return jax.nn.silu(x)

def _sigmoid(x):
    return jax.nn.sigmoid(x)

def _layernorm(x, axis=-1, eps=1e-05):
    m = jnp.mean(x, axis=axis, keepdims=True)
    v = jnp.var(x, axis=axis, keepdims=True)
    return (x - m) / jnp.sqrt(v + eps)

def _scatter_add(tgt, idx, src, axis=0):
    return tgt.at[idx].add(src)

def _segment_sum(src, seg, n):
    return jax.ops.segment_sum(src, seg, n)
kernel_name = 'mk_adaln_d2_jaxref_r4_631f07'

def setup_inputs(seed: int=0):
    np.random.seed(seed)
    _w = jnp.asarray

    def _L0_attn_setup():
        import jax, jax.numpy as jnp
        import numpy as np
        import math
        DIM_EMBD = 256
        N_HEADS = 16
        DIM_HEAD = DIM_EMBD // N_HEADS
        LAMBDA_INIT = 0.8
        EPS = 1e-05
        key = jax.random.key(seed)
        ks = jax.random.split(key, 9)
        B, N = (2, 512)
        d2 = 2 * DIM_HEAD * N_HEADS
        xavier = lambda k, shp: jax.random.uniform(k, shp, jnp.float32, -1.0, 1.0) * math.sqrt(6.0 / (shp[0] + shp[1]))
        return {'X': jax.random.normal(ks[0], (B, N, DIM_EMBD), jnp.float32), 'W_q': xavier(ks[1], (d2, DIM_EMBD)), 'W_k': xavier(ks[2], (d2, DIM_EMBD)), 'W_v': xavier(ks[3], (d2, DIM_EMBD)), 'W_o': xavier(ks[4], (DIM_EMBD, d2)), 'lambda_q1': jax.random.normal(ks[5], (N_HEADS, DIM_HEAD), jnp.float32), 'lambda_k1': jax.random.normal(ks[6], (N_HEADS, DIM_HEAD), jnp.float32), 'lambda_q2': jax.random.normal(ks[7], (N_HEADS, DIM_HEAD), jnp.float32), 'lambda_k2': jax.random.normal(ks[8], (N_HEADS, DIM_HEAD), jnp.float32), 'rms_scale': jnp.ones((2 * DIM_HEAD,), jnp.float32)}
    _L0_attn_in = _L0_attn_setup()

    def _L0_ffn_setup():
        import jax, jax.numpy as jnp
        import numpy as np
        NUM_EXPERTS = 8
        CAPACITY = 1024
        key = jax.random.key(seed)
        ks = jax.random.split(key, 5)
        dim, hidden = (256, 512)
        x = jax.random.normal(ks[0], (4, 1024, dim), dtype=jnp.float32)
        wg = jax.random.normal(ks[1], (dim, NUM_EXPERTS), dtype=jnp.float32) * 0.02
        w1 = jax.random.normal(ks[2], (NUM_EXPERTS, dim, hidden), dtype=jnp.float32) * 0.02
        w3 = jax.random.normal(ks[3], (NUM_EXPERTS, dim, hidden), dtype=jnp.float32) * 0.02
        w2 = jax.random.normal(ks[4], (NUM_EXPERTS, hidden, dim), dtype=jnp.float32) * 0.02
        return {'x': x, 'wg': wg, 'w1': w1, 'w3': w3, 'w2': w2}
    _L0_ffn_in = _L0_ffn_setup()
    _L0_c = _w((lambda *s: np.random.randn(*s).astype(np.float32) * 0.05)(2, 256))
    _L0_wmod = _w((lambda *s: np.random.randn(*s).astype(np.float32) * 0.05)(256, 6 * 256) * 256 ** (-0.5))

    def _L1_attn_setup():
        import jax, jax.numpy as jnp
        import numpy as np
        B, T, E, H = (2, 1024, 256, 16)
        D = E // H
        EPS = 1e-06

        def _feature_map(x):
            return jnp.where(x > 0, x + 1.0, jnp.exp(x))
        key = jax.random.key(seed)
        ks = jax.random.split(key, 9)
        s = 1.0 / np.sqrt(E)
        return {'x': jax.random.normal(ks[0], (B, T, E), dtype=jnp.float32), 'wq': jax.random.uniform(ks[1], (E, E), jnp.float32, -s, s), 'bq': jax.random.uniform(ks[2], (E,), jnp.float32, -s, s), 'wk': jax.random.uniform(ks[3], (E, E), jnp.float32, -s, s), 'bk': jax.random.uniform(ks[4], (E,), jnp.float32, -s, s), 'wv': jax.random.uniform(ks[5], (E, E), jnp.float32, -s, s), 'bv': jax.random.uniform(ks[6], (E,), jnp.float32, -s, s), 'wo': jax.random.uniform(ks[7], (E, E), jnp.float32, -s, s), 'bo': jax.random.uniform(ks[8], (E,), jnp.float32, -s, s)}
    _L1_attn_in = _L1_attn_setup()

    def _L1_ffn_setup():
        import jax, jax.numpy as jnp
        import numpy as np
        CAPACITY_FACTOR = 1.0

        def _top1_gate(x2d, wg):
            S, _ = x2d.shape
            E = wg.shape[1]
            C = int(CAPACITY_FACTOR * S / E)
            logits = x2d @ wg
            gates = jax.nn.softmax(logits, axis=-1)
            idx = jnp.argmax(gates, axis=-1)
            mask = jax.nn.one_hot(idx, E, dtype=jnp.int32)
            loc = jnp.cumsum(mask, axis=0) - 1
            me = jnp.mean(gates, axis=0)
            ce = jnp.mean(mask.astype(gates.dtype), axis=0)
            l_aux = E * jnp.sum(me * ce)
            mask = mask * (loc < C).astype(jnp.int32)
            gate_s = jnp.sum(gates * mask, axis=-1)
            loc_s = jnp.sum(loc * mask, axis=-1)
            loc_oh = jax.nn.one_hot(loc_s, C, dtype=gates.dtype)
            combine = (gate_s[:, None] * mask.astype(gates.dtype))[:, :, None] * loc_oh[:, None, :]
            dispatch = (combine > 0).astype(gates.dtype)
            return (l_aux, combine, dispatch)
        key = jax.random.key(seed)
        k1, k2, k3, k4 = jax.random.split(key, 4)
        s, b, m, E, ffn = (512, 4, 256, 8, 1024)
        x = jax.random.normal(k1, (s, b, m), dtype=jnp.float32)
        wg = jax.random.normal(k2, (m, E), dtype=jnp.float32) * 0.02
        w1 = jax.random.normal(k3, (E, m, ffn), dtype=jnp.float32) * 0.02
        w2 = jax.random.normal(k4, (E, ffn, m), dtype=jnp.float32) * 0.02
        return {'x': x, 'wg': wg, 'w1': w1, 'w2': w2}
    _L1_ffn_in = _L1_ffn_setup()
    _L1_c = _w((lambda *s: np.random.randn(*s).astype(np.float32) * 0.05)(2, 256))
    _L1_wmod = _w((lambda *s: np.random.randn(*s).astype(np.float32) * 0.05)(256, 6 * 256) * 256 ** (-0.5))
    _d = {'L0_attn_X': _L0_attn_in['X'], 'L0_attn_W_q': _L0_attn_in['W_q'], 'L0_attn_W_k': _L0_attn_in['W_k'], 'L0_attn_W_v': _L0_attn_in['W_v'], 'L0_attn_W_o': _L0_attn_in['W_o'], 'L0_attn_lambda_q1': _L0_attn_in['lambda_q1'], 'L0_attn_lambda_k1': _L0_attn_in['lambda_k1'], 'L0_attn_lambda_q2': _L0_attn_in['lambda_q2'], 'L0_attn_lambda_k2': _L0_attn_in['lambda_k2'], 'L0_attn_rms_scale': _L0_attn_in['rms_scale'], 'L0_ffn_wg': _L0_ffn_in['wg'], 'L0_ffn_w1': _L0_ffn_in['w1'], 'L0_ffn_w3': _L0_ffn_in['w3'], 'L0_ffn_w2': _L0_ffn_in['w2'], 'L0_c': _L0_c, 'L0_wmod': _L0_wmod, 'L1_attn_wq': _L1_attn_in['wq'], 'L1_attn_bq': _L1_attn_in['bq'], 'L1_attn_wk': _L1_attn_in['wk'], 'L1_attn_bk': _L1_attn_in['bk'], 'L1_attn_wv': _L1_attn_in['wv'], 'L1_attn_bv': _L1_attn_in['bv'], 'L1_attn_wo': _L1_attn_in['wo'], 'L1_attn_bo': _L1_attn_in['bo'], 'L1_ffn_wg': _L1_ffn_in['wg'], 'L1_ffn_w1': _L1_ffn_in['w1'], 'L1_ffn_w2': _L1_ffn_in['w2'], 'L1_c': _L1_c, 'L1_wmod': _L1_wmod}
    _x0 = _d['L0_attn_X']
    _d['L0_attn_X'] = jax.random.normal(jax.random.fold_in(jax.random.key(seed), 1), (2, 2048, 256), dtype=_x0.dtype)
    del _x0
    return _d

def reference(L0_attn_X, L0_attn_W_q, L0_attn_W_k, L0_attn_W_v, L0_attn_W_o, L0_attn_lambda_q1, L0_attn_lambda_k1, L0_attn_lambda_q2, L0_attn_lambda_k2, L0_attn_rms_scale, L0_ffn_wg, L0_ffn_w1, L0_ffn_w3, L0_ffn_w2, L0_c, L0_wmod, L1_attn_wq, L1_attn_bq, L1_attn_wk, L1_attn_bk, L1_attn_wv, L1_attn_bv, L1_attn_wo, L1_attn_bo, L1_ffn_wg, L1_ffn_w1, L1_ffn_w2, L1_c, L1_wmod):

    def _L0_attn_ref(X, W_q, W_k, W_v, W_o, lambda_q1, lambda_k1, lambda_q2, lambda_k2, rms_scale):
        import jax, jax.numpy as jnp
        import numpy as np
        import math
        DIM_EMBD = 256
        N_HEADS = 16
        DIM_HEAD = DIM_EMBD // N_HEADS
        LAMBDA_INIT = 0.8
        EPS = 1e-05
        B, N, _ = X.shape
        H, dh = (N_HEADS, DIM_HEAD)

        def split_heads(Y):
            return Y.reshape(B, N, H, 2 * dh).transpose(0, 2, 1, 3)
        Q = split_heads(X @ W_q.T)
        K = split_heads(X @ W_k.T)
        V = split_heads(X @ W_v.T)
        Q1, Q2 = (Q[..., :dh], Q[..., dh:])
        K1, K2 = (K[..., :dh], K[..., dh:])
        lam = jnp.exp(jnp.sum(lambda_q1 * lambda_k1, -1)) - jnp.exp(jnp.sum(lambda_q2 * lambda_k2, -1)) + LAMBDA_INIT
        lam = lam[None, :, None, None]
        scaling = 1.0 / math.sqrt(dh)
        causal = jnp.tril(jnp.ones((N, N), jnp.bool_))
        neg_inf = jnp.float32(-jnp.inf)
        A1 = jnp.einsum('bhqd,bhkd->bhqk', Q1, K1) * scaling
        A2 = jnp.einsum('bhqd,bhkd->bhqk', Q2, K2) * scaling
        A1 = jnp.where(causal, A1, neg_inf)
        A2 = jnp.where(causal, A2, neg_inf)
        attn = jax.nn.softmax(A1, -1) - lam * jax.nn.softmax(A2, -1)
        O = jnp.einsum('bhqk,bhkd->bhqd', attn, V)
        rms = jnp.sqrt(jnp.mean(O * O, -1, keepdims=True) + EPS)
        O = O / rms * rms_scale * (1.0 - LAMBDA_INIT)
        O = O.transpose(0, 2, 1, 3).reshape(B, N, H * 2 * dh)
        return O @ W_o.T

    def _L0_ffn_ref(x, wg, w1, w3, w2):
        import jax, jax.numpy as jnp
        import numpy as np
        NUM_EXPERTS = 8
        CAPACITY = 1024
        bz, slen, dim = x.shape
        xt = x.reshape(bz * slen, dim)
        scores = jax.nn.softmax(xt @ wg, axis=-1)
        top_scores, sel = jax.lax.top_k(scores.T, CAPACITY)
        token_idx = sel.reshape(-1)
        routed = xt[token_idx] * top_scores.reshape(-1, 1)
        routed = routed.reshape(NUM_EXPERTS, CAPACITY, dim)
        h = jax.nn.silu(jnp.einsum('ecd,edh->ech', routed, w1)) * jnp.einsum('ecd,edh->ech', routed, w3)
        routed_out = jnp.einsum('ech,ehd->ecd', h, w2).reshape(-1, dim)
        out = jnp.zeros_like(xt).at[token_idx].add(routed_out)
        return out.reshape(bz, slen, dim)

    def _L1_attn_ref(x, wq, bq, wk, bk, wv, bv, wo, bo):
        import jax, jax.numpy as jnp
        import numpy as np
        B, T, E, H = (2, 1024, 256, 16)
        D = E // H
        EPS = 1e-06

        def _feature_map(x):
            return jnp.where(x > 0, x + 1.0, jnp.exp(x))
        b, t, e = x.shape
        q = _feature_map(x @ wq + bq).reshape(b, t, H, D)
        k = _feature_map(x @ wk + bk).reshape(b, t, H, D)
        v = (x @ wv + bv).reshape(b, t, H, D)
        qT = jnp.moveaxis(q, 1, 0)
        kT = jnp.moveaxis(k, 1, 0)
        vT = jnp.moveaxis(v, 1, 0)
        S0 = jnp.zeros((b, H, D, D), dtype=x.dtype)
        z0 = jnp.zeros((b, H, D), dtype=x.dtype)

        def step(carry, qkv):
            S, z = carry
            qt, kt, vt = qkv
            S = S + jnp.einsum('bhd,bhe->bhde', kt, vt)
            z = z + kt
            num = jnp.einsum('bhd,bhde->bhe', qt, S)
            den = jnp.einsum('bhd,bhd->bh', qt, z)[..., None] + EPS
            return ((S, z), num / den)
        _, outT = jax.lax.scan(step, (S0, z0), (qT, kT, vT))
        out = jnp.moveaxis(outT, 0, 1).reshape(b, t, e)
        return out @ wo + bo

    def _L1_ffn_ref(x, wg, w1, w2):
        import jax, jax.numpy as jnp
        import numpy as np
        CAPACITY_FACTOR = 1.0

        def _top1_gate(x2d, wg):
            S, _ = x2d.shape
            E = wg.shape[1]
            C = int(CAPACITY_FACTOR * S / E)
            logits = x2d @ wg
            gates = jax.nn.softmax(logits, axis=-1)
            idx = jnp.argmax(gates, axis=-1)
            mask = jax.nn.one_hot(idx, E, dtype=jnp.int32)
            loc = jnp.cumsum(mask, axis=0) - 1
            me = jnp.mean(gates, axis=0)
            ce = jnp.mean(mask.astype(gates.dtype), axis=0)
            l_aux = E * jnp.sum(me * ce)
            mask = mask * (loc < C).astype(jnp.int32)
            gate_s = jnp.sum(gates * mask, axis=-1)
            loc_s = jnp.sum(loc * mask, axis=-1)
            loc_oh = jax.nn.one_hot(loc_s, C, dtype=gates.dtype)
            combine = (gate_s[:, None] * mask.astype(gates.dtype))[:, :, None] * loc_oh[:, None, :]
            dispatch = (combine > 0).astype(gates.dtype)
            return (l_aux, combine, dispatch)
        s, b, m = x.shape
        x2d = x.reshape(-1, m)
        l_aux, combine, dispatch = _top1_gate(x2d, wg)
        combine = combine[:, None]
        dispatch = dispatch[:, None]
        xr = x2d[:, None, :]
        dispatched = jnp.einsum('szfc,szm->zfcm', dispatch, xr)
        E = w1.shape[0]
        di = dispatched.reshape(E, -1, m)
        h = jax.nn.relu(jnp.einsum('ecm,emh->ech', di, w1))
        eo = jnp.einsum('ech,ehm->ecm', h, w2)
        eo = eo[None]
        out = jnp.einsum('szfc,zfcm->sm', combine, eo)
        return out.reshape(s, b, m)
    x = L0_attn_X
    mod = (_silu(L0_c) @ L0_wmod).reshape(L0_c.shape[0], 6, 1, -1)
    sa, ca, ga, sb, cb, gb = (mod[:, 0], mod[:, 1], mod[:, 2], mod[:, 3], mod[:, 4], mod[:, 5])
    ga = (2 * (ga >= 0) - 1) * jnp.maximum(jnp.abs(ga), 0.25)
    gb = (2 * (gb >= 0) - 1) * jnp.maximum(jnp.abs(gb), 0.25)
    h = _layernorm(x, axis=-1) * (1 + ca) + sa
    x = x + ga * _L0_attn_ref(h, L0_attn_W_q, L0_attn_W_k, L0_attn_W_v, L0_attn_W_o, L0_attn_lambda_q1, L0_attn_lambda_k1, L0_attn_lambda_q2, L0_attn_lambda_k2, L0_attn_rms_scale)
    h = _layernorm(x, axis=-1) * (1 + cb) + sb
    x = x + gb * _L0_ffn_ref(h, L0_ffn_wg, L0_ffn_w1, L0_ffn_w3, L0_ffn_w2)
    mod = (_silu(L1_c) @ L1_wmod).reshape(L1_c.shape[0], 6, 1, -1)
    sa, ca, ga, sb, cb, gb = (mod[:, 0], mod[:, 1], mod[:, 2], mod[:, 3], mod[:, 4], mod[:, 5])
    ga = (2 * (ga >= 0) - 1) * jnp.maximum(jnp.abs(ga), 0.25)
    gb = (2 * (gb >= 0) - 1) * jnp.maximum(jnp.abs(gb), 0.25)
    h = _layernorm(x, axis=-1) * (1 + ca) + sa
    x = x + ga * _L1_attn_ref(h, L1_attn_wq, L1_attn_bq, L1_attn_wk, L1_attn_bk, L1_attn_wv, L1_attn_bv, L1_attn_wo, L1_attn_bo)
    h = _layernorm(x, axis=-1) * (1 + cb) + sb
    x = x + gb * _L1_ffn_ref(h, L1_ffn_wg, L1_ffn_w1, L1_ffn_w2)
    return x

_drawn_inputs = setup_inputs


def setup_inputs(seed=0):
    import zlib

    import numpy as np

    out = dict(_drawn_inputs(seed))
    spreads = {'L0_attn_rms_scale': (1.0, 0.6)}
    factors = {'L0_attn_lambda_q1': 2.865,
     'L0_ffn_wg': 8.0,
     'L0_ffn_w1': 8.0,
     'L0_ffn_w3': 8.0,
     'L0_ffn_w2': 8.0,
     'L1_attn_wq': 8.0,
     'L1_attn_bq': 8.0,
     'L1_attn_wk': 8.0,
     'L1_attn_bk': 21.696,
     'L1_attn_wv': 8.0,
     'L1_attn_bv': 8.0,
     'L1_attn_wo': 6.829,
     'L1_attn_bo': 6.436,
     'L1_ffn_wg': 8.0,
     'L1_ffn_w1': 8.0,
     'L1_ffn_w2': 8.0,
     'L1_c': 4.024,
     'L1_wmod': 4.316}
    for name, (base, spread) in spreads.items():
        noise = np.random.default_rng([zlib.crc32(name.encode()), seed]).standard_normal(out[name].shape)
        drawn = base * np.exp(spread * noise) if base else spread * noise
        out[name] = jnp.asarray(drawn.astype(out[name].dtype))
    for name, factor in factors.items():
        out[name] = (out[name] * factor).astype(out[name].dtype)
    return out
```

```python
from contextlib import ExitStack

import concourse.bass as bass
from concourse import mybir

F32 = mybir.dt.float32
BF16 = mybir.dt.bfloat16
I32 = mybir.dt.int32
ALU = mybir.AluOpType
ACT = mybir.ActivationFunctionType
AX = mybir.AxisListType
ds = bass.ds

P = 128
B, N, D = 2, 2048, 256
S = B * N
T = S // P
DC = D // P
GROUP = 512
GT = GROUP // P
NG = N // GROUP
H = 16
DV = 32
DH = 16
DQ = H * DV
NE = 8
CAP0, CAP1 = 1024, 512
HID0, HID1 = 512, 1024
BIG = 1.0e30
LN_EPS = 1e-5
DEN_EPS = 1e-6
LAMBDA_INIT = 0.8

CONSTS = {}
_at = 0
for _name, _width in (("ident", P), ("ones", P), ("before", P), ("upto", P), ("mask_q", P), ("mask_k", P),
                      ("iota", P), ("part", 1), ("headof", NE), ("blockdiag", NE * 17), ("tile_of", T * NE),
                      ("expert", NE), ("expert_base", NE), ("fold", 2 * H)):
    CONSTS[_name] = (_at, _at + _width)
    _at += _width
N_CONSTS = _at


def constants(np):
    c = np.zeros((P, N_CONSTS), np.float32)

    def put(name, value):
        a, b = CONSTS[name]
        c[:, a:b] = value

    p, m = np.arange(P)[:, None], np.arange(P)[None, :]
    put("ident", p == m)
    put("ones", 1.0)
    put("before", p < m)
    put("upto", p <= m)
    put("mask_q", np.where(m > p, -BIG, 0.0))
    put("mask_k", np.where(p > m, -BIG, 0.0))
    put("iota", m)
    put("part", p)
    put("headof", p // DH == np.arange(NE)[None, :])
    put("blockdiag", np.repeat(p // DH == np.arange(NE)[None, :], 17, axis=1))
    put("tile_of", np.repeat(np.arange(T), NE)[None, :])
    put("expert", np.arange(NE)[None, :])
    put("expert_base", np.arange(NE)[None, :] * CAP1)
    put("fold", (p < 4 * H) & (p // 4 * 2 + p % 2 == np.arange(2 * H)[None, :]))
    return c


def wait_apart(engine, sem, value, passed):
    engine.wait_ge(sem, value)
    engine.sem_inc(passed, 1)


class Counted:

    def __init__(self, engine, sem, base=0):
        self.engine, self.sem, self.base, self.n = engine, sem, base, 0

    def then(self, instruction):
        self.n += 1
        instruction.then_inc(self.sem, 1)
        self.engine.wait_ge(self.sem, self.base + self.n)

    def then_apart(self, instruction, passed):
        self.n += 1
        instruction.then_inc(self.sem, 1)
        wait_apart(self.engine, self.sem, self.base + self.n, passed)


class Core:

    def __init__(self, nc, ctx):
        self.nc, self.ctx = nc, ctx
        sb = self.sb
        self.x = sb("x", [P, T, D], F32)
        self.consts = sb("consts", [P, N_CONSTS], F32)
        self.ident_bf = sb("ident_bf", [P, P], BF16)
        self.mask_q_bf = sb("mask_q_bf", [P, P], BF16)
        self.mask_k_bf = sb("mask_k_bf", [P, P], BF16)
        self.pre = sb("pre", [P, 2, 2 * DC, B], F32)
        self.rows = sb("rows", [P, 2, B, 4, D], F32)
        self.passed = ctx.enter_context(nc.semaphore("passed"))

    def sb(self, name, shape, dtype):
        return self.ctx.enter_context(self.nc.sbuf_tensor(name, shape, dtype))

    def c(self, name):
        a, b = CONSTS[name]
        return self.consts[:, a:b]


GATE_A, SHIFT_B, SCALE_B, GATE_B = range(4)


class stage(ExitStack):

    def __init__(self, nc, name):
        super().__init__()
        self.nc, self.name, self.sems = nc, name, []

    def sb(self, n, shape, dtype):
        return self.enter_context(self.nc.sbuf_tensor(f"{self.name}_{n}", shape, dtype))

    def ps(self, n, shape, dtype=F32):
        return self.enter_context(self.nc.psum_tensor(f"{self.name}_{n}", shape, dtype))

    def sem(self, n):
        self.sems.append(self.enter_context(self.nc.semaphore(f"{self.name}_{n}")))
        return self.sems[-1]

    def engines(self):
        self.callback(self.clear)
        return self.enter_context(self.nc.Block())

    def clear(self):
        with self.nc.Block() as block:
            @block.gpsimd
            def _(pool):
                for sem in self.sems:
                    pool.sem_clear(sem)


def setup(nc, core, X, consts, cT, wmod):
    with stage(nc, "setup") as s:
        w = s.sb("wmod_sb", [P, 2, DC, 6 * D], F32)
        c = s.sb("c_sb", [P, 2, DC, B], F32)
        e = s.sb("c_exp", [P, 2, DC, B], F32)
        silu = s.sb("c_silu", [P, 2, DC, B], F32)
        wide = s.sb("c_wide", [P, 2, DC, B, P], F32)
        sign = s.sb("gate_sign", [P, D], F32)
        gate = s.sb("gate_abs", [P, D], F32)
        ps_row = [s.ps(f"ps_row{i}", [P, GROUP]) for i in range(4)]
        ps_pre = s.ps("ps_pre", [P, 2, 2 * DC, B])
        x_in, small_in, w_in, c_exp, steps, silu_ok, row_ok, row_used, pre_ok = (
            s.sem(n) for n in ("x_in", "small_in", "w_in", "c_exp_ok", "setup_steps", "silu_ok", "row_ok",
                               "row_used", "pre_ok"))
        block = s.engines()
        units = [(layer, b, half) for layer in range(2) for b in range(B) for half in range(2)]

        @block.sync
        def _(sp):
            for layer in range(2):
                sp.dma_start(c[:, layer], cT[layer].rearrange("(k p) b -> p k b", p=P)).then_inc(small_in, 16)
            sp.dma_start(core.consts[:], consts).then_inc(small_in, 16)
            for layer in range(2):
                sp.dma_start(w[:, layer], wmod[layer].rearrange("(k p) n -> p k n", p=P)).then_inc(w_in, 16)
            sp.dma_start(core.x[:], X.rearrange("b (t p) d -> p (b t) d", p=P)).then_inc(x_in, 16)
            sp.wait_ge(x_in, 16)

        @block.scalar
        def _(act):
            act.wait_ge(small_in, 48)
            act.activation(e[:], c[:], ACT.Exp, scale=-1.0).then_inc(c_exp, 1)

        @block.vector
        def _(dve):
            link = Counted(dve, steps).then
            dve.wait_ge(small_in, 48)
            dve.tensor_copy(core.ident_bf[:], core.c("ident"))
            dve.tensor_copy(core.mask_q_bf[:], core.c("mask_q"))
            dve.tensor_copy(core.mask_k_bf[:], core.c("mask_k"))
            dve.wait_ge(c_exp, 1)
            link(dve.tensor_scalar(e[:], e[:], 1.0, None, ALU.add))
            link(dve.reciprocal(e[:], e[:]))
            link(dve.tensor_tensor(silu[:], c[:], e[:], ALU.mult))
            flat = silu[:].rearrange("p l k b -> p (l k b)")
            dve.tensor_copy(wide[:].rearrange("p l k b m -> p (l k b) m"),
                            flat.unsqueeze(2).broadcast_to([P, 2 * DC * B, P])).then_inc(silu_ok, 1)
            dve.wait_ge(pre_ok, 1)
            dve.tensor_copy(core.pre[:, :, 0:DC], ps_pre[:, :, 0:DC])
            dve.tensor_scalar(core.pre[:, :, DC:], ps_pre[:, :, DC:], 1.0, None, ALU.add)
            for n, (layer, b, half) in enumerate(units):
                dve.wait_ge(row_ok, n + 1)
                psum, row = ps_row[n % 4], core.rows[:, layer, b]
                at = 0 if half == 0 else D
                link(dve.tensor_scalar(sign[:], psum[:, at:at + D], 0.0, 2.0, ALU.is_ge, ALU.mult))
                link(dve.tensor_scalar(sign[:], sign[:], -1.0, None, ALU.add))
                link(dve.tensor_tensor(gate[:], psum[:, at:at + D], sign[:], ALU.mult))
                link(dve.tensor_scalar(gate[:], gate[:], 0.25, None, ALU.max))
                link(dve.tensor_tensor(row[:, GATE_A if half == 0 else GATE_B], gate[:], sign[:], ALU.mult))
                if half == 0:
                    last = dve.tensor_copy(row[:, SHIFT_B], psum[:, D:2 * D])
                else:
                    last = dve.tensor_scalar(row[:, SCALE_B], psum[:, 0:D], 1.0, None, ALU.add)
                last.then_inc(row_used, 1)

        @block.tensor
        def _(pe):
            pe.wait_ge(silu_ok, 1)
            pe.wait_ge(w_in, 32)
            for layer in range(2):
                for m in range(2 * DC):
                    for k in range(DC):
                        last = pe.matmul(ps_pre[:, layer, m], w[:, layer, k, m * P:(m + 1) * P], silu[:, layer, k],
                                         start=(k == 0), stop=(k == DC - 1))
            last.then_inc(pre_ok, 1)
            for n, (layer, b, half) in enumerate(units):
                if n >= 4:
                    pe.wait_ge(row_used, n - 3)
                for k in range(DC):
                    last = pe.matmul(ps_row[n % 4][:], wide[:, layer, k, b],
                                     w[:, layer, k, (half + 1) * GROUP:(half + 2) * GROUP],
                                     start=(k == 0), stop=(k == DC - 1))
                last.then_inc(row_ok, 1)


def norm_statistics(dve, chain, core, g, mv, stats, rstd, var_ok, std_ok):
    for j in range(GT):
        last = dve.bn_stats(stats[:, j], core.x[:, ds(g * GT + j, 1), :])
    chain.then_apart(last, core.passed)
    for j in range(GT):
        last = dve.bn_aggr(mv[:, j], stats[:, j])
    chain.then(last)
    dve.tensor_scalar(mv[:, :, 1], mv[:, :, 1], LN_EPS, None, ALU.add).then_inc(var_ok, 1)
    dve.wait_ge(std_ok, g + 1)
    chain.then(dve.reciprocal(rstd[:], rstd[:]))


def group_norm(dve, chain, core, g, mv, stats, rstd, normed, var_ok, std_ok, normed_free):
    norm_statistics(dve, chain, core, g, mv, stats, rstd, var_ok, std_ok)
    if normed_free is not None:
        dve.wait_ge(*normed_free)
    for j in range(GT):
        last = dve.tensor_scalar(normed[:, j:j + 1, :], core.x[:, ds(g * GT + j, 1), :], mv[:, j, 0:1],
                                 rstd[:, j:j + 1], ALU.subtract, ALU.mult)
    return last


NORM_LINKS = 3


def run_ahead(engine, step):
    for b in range(B):
        last = (b + 1) * NG - 1
        with engine.Fori(b * NG, last) as g:
            step(b, g, b, g + 1)
        step(b, last, b + 1, last + 1 if b + 1 < B else None)


def project0(nc, core, wT, qk_parts, v):
    with stage(nc, "project0") as s:
        w = s.sb("wqkv", [P, 3, DC, DQ], F32)
        stats = s.sb("stats", [P, GT, 6], F32)
        mv = s.sb("mean_var", [P, GT, 2], F32)
        rstd = s.sb("rstd", [P, GT], F32)
        normed = s.sb("normed", [P, GT, D], F32)
        hT = s.sb("hT", [P, DC, GROUP], F32)
        SLOTS = 4
        parts = s.sb("parts", [P, SLOTS, 3, GROUP], BF16)
        rest = s.sb("rest", [P, SLOTS, GROUP], F32)
        ps_t = s.ps("ps_t", [P, DC, GROUP])
        RING = 6
        ps_o = [s.ps(f"ps_o{i}", [P, GROUP]) for i in range(RING)]
        QK = 2 * DQ // P
        OUTS = QK + GT
        names = ("w_in", "steps", "var_ok", "std_ok", "normed_ok", "turned", "hT_ok",
                 "out_ok", "out_used", "hi_ok", "rest_ok", "mid_ok", "parts_ok")
        (w_in, steps, var_ok, std_ok, normed_ok, turned, hT_ok, out_ok, out_used, hi_ok,
         rest_ok, mid_ok, parts_ok) = (s.sem(n) for n in names)
        stored = [s.sem(f"stored{i}") for i in range(SLOTS)]
        block = s.engines()

        assert QK - RING == 2 and OUTS == 2 * RING

        @block.sync
        def _(sp):
            for n in range(3):
                sp.dma_start(w[:, n], wT[n].rearrange("(k p) n -> p k n", p=P)).then_inc(w_in, 16)
            sp.wait_ge(w_in, 48)
            for slot in range(SLOTS):
                sp.sem_inc(stored[slot], 16)
            for b in range(B):
                with sp.Fori(b * NG, (b + 1) * NG) as g:
                    at = sp.snap((g - b * NG) * GROUP)
                    for o in range(QK):
                        which, head = o // 4, b * H + (o % 4) * 4
                        wait_apart(sp, parts_ok, g * QK + o + 1 + SLOTS, core.passed)
                        sp.dma_start(qk_parts[:, which, head:head + 4, :, ds(at, GROUP)].rearrange(
                            "s n d t -> (n d) s t"), parts[:, o % SLOTS]).then_inc(stored[o % SLOTS], 16)
            for slot in range(SLOTS):
                sp.wait_ge(stored[slot], (B * NG * QK // SLOTS + 1) * 16)

        @block.scalar
        def _(act):
            def root(g):
                act.wait_ge(var_ok, g + 1)
                act.activation(rstd[:], mv[:, :, 1], ACT.Sqrt).then_inc(std_ok, 1)

            def step(b, g, next_b, after):
                act.wait_ge(turned, g + 1)
                act.wait_ge(out_ok, g * OUTS + 1)
                for k in range(DC):
                    act.activation(hT[:, k], ps_t[:, k], ACT.Identity, scale=core.pre[:, 0, DC + k, b:b + 1],
                                   bias=core.pre[:, 0, k, b:b + 1]).then_inc(hT_ok, 1)
                for o in range(QK + 1):
                    if o < QK:
                        act.wait_ge(out_ok, g * OUTS + o + 2)
                        act.wait_ge(stored[o % SLOTS], (g * (QK // SLOTS) + o // SLOTS + 1) * 16)
                        act.activation(parts[:, o % SLOTS, 0], ps_o[o % RING][:], ACT.Copy).then_inc(hi_ok, 1)
                    if o > 0:
                        slot = (o - 1) % SLOTS
                        act.wait_ge(rest_ok, g * QK + o + 2)
                        act.activation(parts[:, slot, 1], rest[:, slot], ACT.Copy).then_inc(mid_ok, 1)
                if after is not None:
                    root(after)

            root(0)
            run_ahead(act, step)

        @block.gpsimd
        def _(pool):
            pool.sem_inc(parts_ok, SLOTS)

            def step(b, g, next_b, after):
                for o in range(QK):
                    pool.wait_ge(mid_ok, g * QK + o + 1)
                    pool.tensor_tensor(parts[:, o % SLOTS, 2], rest[:, o % SLOTS], parts[:, o % SLOTS, 1],
                                       ALU.subtract).then_inc(parts_ok, 1)

            run_ahead(pool, step)

        @block.vector
        def _(dve):
            dve.sem_inc(rest_ok, 2)
            dve.sem_inc(out_used, GT)

            def norm(g):
                chain = Counted(dve, steps, g * NORM_LINKS)
                group_norm(dve, chain, core, g, mv, stats, rstd, normed, var_ok, std_ok, None).then_inc(normed_ok, 1)

            def step(b, g, next_b, after):
                for o in range(QK):
                    dve.wait_ge(hi_ok, g * QK + o + 1)
                    dve.wait_ge(parts_ok, g * QK + o + 1)
                    dve.tensor_tensor(rest[:, o % SLOTS], ps_o[o % RING][:], parts[:, o % SLOTS, 0], ALU.subtract)\
                        .then_inc(rest_ok, 1)
                if after is not None:
                    norm(after)
                for j in range(GT):
                    o = QK + j
                    dve.wait_ge(out_ok, g * OUTS + o + 2)
                    dve.tensor_copy(v[:, b * H:(b + 1) * H, ds((g - b * NG) * GT + j, 1), :],
                                    ps_o[o % RING][:].rearrange("p (h a e) -> p h a e", h=H, a=1))\
                        .then_inc(out_used, 1)

            norm(0)
            run_ahead(dve, step)

        @block.tensor
        def _(pe):
            pe.sem_inc(out_ok, 1)
            pe.wait_ge(w_in, 48)

            def turn(g):
                pe.wait_ge(normed_ok, g + 1)
                for k in range(DC):
                    for j in range(GT):
                        last = pe.transpose(ps_t[:, k, j * P:(j + 1) * P], normed[:, j, k * P:(k + 1) * P],
                                            core.c("ident"))
                last.then_inc(turned, 1)

            def step(b, g, next_b, after):
                pe.wait_ge(hT_ok, (g + 1) * DC)
                for o in range(OUTS):
                    if after is not None and o == OUTS - 2:
                        turn(after)
                    if o < 2:
                        pe.wait_ge(rest_ok, g * QK + o + 1)
                    elif o < RING:
                        pe.wait_ge(out_used, g * GT + o - 1)
                    else:
                        pe.wait_ge(rest_ok, g * QK + o - RING + 3)
                    for k in range(DC):
                        if o < QK:
                            last = pe.matmul(ps_o[o % RING][:], w[:, o // 4, k, (o % 4) * P:(o % 4 + 1) * P],
                                             hT[:, k], start=(k == 0), stop=(k == DC - 1))
                        else:
                            j = o - QK
                            last = pe.matmul(ps_o[o % RING][:], hT[:, k, j * P:(j + 1) * P], w[:, 2, k],
                                             start=(k == 0), stop=(k == DC - 1))
                    last.then_inc(out_ok, 1)

            turn(0)
            run_ahead(pe, step)


STRIPS = ((0, 0), (1, 1), (2, 0), (0, 1), (0, 2), (1, 0))
RUNS = (((0, 0, 3), (3, 0, 1), (4, 0, 2)), ((0, 0, 2), (2, 0, 3), (5, 0, 1)))
assert all([strip[which] for strip in STRIPS] == [part + n for _, part, count in RUNS[which] for n in range(count)]
           for which in range(2))
STACK = len(STRIPS) * DH
WITH_MAX = STACK + 3
HEADS = B * H
Q_TILES = N // GROUP
K_TILES = N // P
TURNS = tuple(range(Q_TILES))
STEPS = [(turn, tq, kb) for turn, tq in enumerate(TURNS) for kb in range(GT * (tq + 1))]
QUAD = 4
MAXIMA = [(a, jq, c) for a in range(2) for jq in range(K_TILES) for c in range(jq // GT + 1)]
FIRST_MAX, LAST_MAX, TURN_MAX = 2, 32, 32


def is_first(head):
    return isinstance(head, int) and head == 0


def attention0(nc, core, qk_parts, v, oT, sums):
    with stage(nc, "attention0") as s:
        RING_P, RING_S, RING_M, RING_O = 2 * QUAD, 3, 3, 2
        qs = [s.sb(f"q_stack{i}", [P, 2, N], BF16) for i in range(2)]
        ks = [s.sb(f"k_stack{i}", [P, 2, N], BF16) for i in range(2)]
        vh = [s.sb(f"v_head{i}", [P, K_TILES, DV], F32) for i in range(2)]
        probs = s.sb("probs", [P, RING_P, 2, GROUP], F32)
        even = s.sb("even_sb", [2 * DV, RING_O, GROUP], F32)
        odd = s.sb("odd_sb", [2 * DV, RING_O, GROUP], F32)
        out = s.sb("out_sb", [2 * DV, RING_O, GROUP], F32)
        total = s.sb("total_sb", [P, RING_O, GROUP], F32)
        zeros = s.sb("zeros", [P, P + GROUP], BF16)
        chunk_max = s.sb("chunk_max", [P, 2, K_TILES, Q_TILES], F32)
        neg_max = s.sb("neg_max", [P, 2 * K_TILES], F32)
        max_parts = s.sb("max_parts", [2 * K_TILES, 3, P], BF16)
        max_rest = s.sb("max_rest", [2 * K_TILES, P], F32)
        ps_s = [s.ps(f"ps_s{i}", [P, GROUP]) for i in range(RING_S)]
        ps_m = [s.ps(f"ps_m{i}", [P, GROUP]) for i in range(RING_M)]
        ps_o = s.ps("ps_o", [P, GROUP])
        ps_l = s.ps("ps_l", [P, GROUP])
        names = ("ready", "score_ok", "prob_ok", "values_ok", "pair_ok", "ones_ok", "max_ok", "max_used", "steps",
                 "neg_ok", "parts_ok", "parts_in", "o_taken", "l_taken", "out_ok", "v_ok")
        (ready, score_ok, prob_ok, values_ok, pair_ok, ones_ok, max_ok, max_used, steps, neg_ok, parts_ok,
         parts_in, o_taken, l_taken, out_ok, v_ok) = (s.sem(n) for n in names)
        loaded = [s.sem(f"loaded{i}") for i in range(2)]
        out_stored = [s.sem(f"out_stored{i}") for i in range(RING_O)]
        total_stored = [s.sem(f"total_stored{i}") for i in range(RING_O)]
        block = s.engines()
        N_STEPS, N_MAX = len(STEPS), len(MAXIMA) + 1
        LOADS = len(RUNS[0]) + len(RUNS[1])
        QUADS = N_STEPS // QUAD
        LAST = [k for k, (_, tq, kb) in enumerate(STEPS) if kb == GT * (tq + 1) - 1]

        def left(k):
            _, tq, kb = STEPS[k]
            return max(0, kb * P - tq * GROUP)

        def width(m):
            a, jq, c = MAXIMA[m]
            return min(GROUP, (jq + 1) * P - c * GROUP)

        def maxima_at(k, alone):
            if alone:
                return range(len(MAXIMA)) if k == 0 else ()
            if not FIRST_MAX <= k < LAST_MAX:
                return ()
            work = [2 * GROUP + left(m) for m in range(FIRST_MAX, LAST_MAX)]
            before, at = sum(work[:k - FIRST_MAX]), work[k - FIRST_MAX]
            return range(before * len(MAXIMA) // sum(work), (before + at) * len(MAXIMA) // sum(work))

        def ends(k, after):
            for turn, end in enumerate(LAST):
                if end + after == k:
                    return turn, False
                if end + after == k + N_STEPS:
                    return turn, True
            return None

        def run(engine, step):
            step(None, 0, 1)
            step(0, 1, 0)
            with engine.Fori(0, HEADS // 2 - 1) as i:
                step(2 * i + 1, 2 * i + 2, 1)
                step(2 * i + 2, 2 * i + 3, 0)
            step(HEADS - 1, None, 1)

        @block.sync
        def _(sp):
            def step(head, after, at):
                other = 1 - at
                if after is not None:
                    nx = after if isinstance(after, int) else sp.snap(after)
                    if head is not None and not is_first(head):
                        wait_apart(sp, score_ok, head * 2 * N_STEPS, core.passed)
                    for which, stack in ((0, qs[other]), (1, ks[other])):
                        for strip, part, count in RUNS[which]:
                            sp.dma_start(stack[strip * DH:(strip + count) * DH].rearrange("p a t -> p (a t)"),
                                         qk_parts[part:part + count, which, ds(nx, 1)].rearrange(
                                             "s n (d a) t -> s (n d) (a t)", a=2)).then_inc(loaded[other], 16)
                for turn in range(Q_TILES):
                    if head is not None and not (is_first(head) and turn == 0):
                        store(head, turn)
                if after is not None:
                    wait_apart(sp, parts_ok, after + 1, core.passed)
                    for part in range(3):
                        sp.dma_start(qs[other][STACK + part:STACK + part + 1].rearrange(
                            "p a (j t) -> p (a j) t", t=P), max_parts[:, part]).then_inc(parts_in, 16)
                else:
                    store(head + 1, 0)

            def store(head, turn):
                tile, slot = TURNS[turn - 1], (turn - 1) % RING_O
                h = head - 1 if turn == 0 else head
                h = h if isinstance(h, int) else sp.snap(h)
                for done, stored, to, results in ((out_ok, out_stored, oT, out[:, slot]),
                                                  (l_taken, total_stored, sums, total[0:P:DV, slot])):
                    wait_apart(sp, done, head * Q_TILES + turn + 1, core.passed)
                    sp.dma_start(to[ds(h, 1), :, tile * GROUP:(tile + 1) * GROUP].rearrange("n e t -> (n e) t"),
                                 results).then_inc(stored[slot], 16)

            for slot in range(RING_O):
                sp.sem_inc(out_stored[slot], 16)
                sp.sem_inc(total_stored[slot], 16)
            sp.sem_inc(parts_in, 48)
            run(sp, step)
            for slot in range(RING_O):
                sp.wait_ge(out_stored[slot], 16 * (1 + HEADS * Q_TILES // RING_O))
                sp.wait_ge(total_stored[slot], 16 * (1 + HEADS * Q_TILES // RING_O))

        @block.gpsimd
        def _(pool):
            def step(head, after, at):
                if after is not None:
                    if head is not None and not is_first(head):
                        wait_apart(pool, values_ok, head * N_STEPS, core.passed)
                    pool.tensor_copy(vh[1 - at][:], v[:, ds(after, 1)]).then_inc(v_ok, 1)
                if head is not None:
                    for k in range(1, N_STEPS, 2):
                        pool.wait_ge(values_ok, head * N_STEPS + k + 1)
                        to, lo = (k - 1) % RING_P, left(k)
                        pool.tensor_tensor(probs[:, to, :, lo:], probs[:, to, :, lo:], probs[:, k % RING_P, :, lo:],
                                           ALU.add).then_inc(pair_ok, 1)

            run(pool, step)

        @block.scalar
        def _(act):
            act.sem_inc(o_taken, 1)
            act.sem_inc(l_taken, 1)

            def take_values(head, turn):
                slot = turn % RING_O
                if not (is_first(head) and turn < RING_O):
                    act.wait_ge(out_ok, head * Q_TILES + turn)
                act.wait_ge(values_ok, head * N_STEPS + LAST[turn] + 1)
                act.activation(odd[:, slot], ps_o[2 * DV:], ACT.Copy)
                act.activation(even[:, slot], ps_o[0:2 * DV], ACT.Copy).then_inc(o_taken, 1)

            def take_total(head, turn):
                slot = turn % RING_O
                if isinstance(head, int):
                    act.wait_ge(total_stored[slot], ((head * Q_TILES + turn) // RING_O + 1) * 16)
                else:
                    act.wait_ge(total_stored[slot], (head * (Q_TILES // RING_O) + turn // RING_O + 1) * 16)
                act.wait_ge(ones_ok, head * QUADS + (LAST[turn] + 1) // QUAD + 2)
                act.activation(total[:, slot], ps_l[:], ACT.Copy).then_inc(l_taken, 1)

            def step(head, after, at):
                if head is None:
                    return
                for k in range(N_STEPS):
                    ended = ends(k, 2)
                    if ended and not (ended[1] and is_first(head)):
                        take_values(head - 1 if ended[1] else head, ended[0])
                    ended = ends(k, QUAD + 1)
                    if ended and not (ended[1] and is_first(head)):
                        take_total(head - 1 if ended[1] else head, ended[0])
                    for a in range(2):
                        act.wait_ge(score_ok, head * 2 * N_STEPS + 2 * k + a + 1)
                        if k % QUAD == 0 and a == 0:
                            act.wait_ge(ones_ok, head * QUADS + k // QUAD + 1)
                        act.activation(probs[:, k % RING_P, a, left(k):], ps_s[(2 * k + a) % RING_S][:, left(k):],
                                       ACT.Exp, scale=float(DH) ** -0.5).then_inc(prob_ok, 1)
                if after is None:
                    take_values(head, Q_TILES - 1)
                    take_total(head, Q_TILES - 1)

            run(act, step)

        @block.vector
        def _(dve):
            for i in range(2):
                dve.memset(ks[i][STACK:P], 1.0)
                dve.memset(qs[i][STACK:P], 0.0)
            dve.memset(zeros[:], 0.0)
            dve.memset(chunk_max[:], -3.0e38).then_inc(ready, 1)
            dve.sem_inc(max_used, RING_M)
            dve.sem_inc(out_ok, 1)
            dve.wait_ge(ready, 1)

            def maxima(after, items):
                for m in items:
                    a, jq, c = MAXIMA[m]
                    dve.wait_ge(max_ok, after * N_MAX + m + 1)
                    last = dve.tensor_reduce(chunk_max[:, a, jq, c:c + 1], ps_m[m % RING_M][:, 0:width(m)], AX.X,
                                             ALU.max)
                    last.then_inc(max_used, 1)
                    if m == len(MAXIMA) - 1:
                        dve.wait_ge(max_used, after * N_MAX + m + 1 + RING_M)
                        dve.tensor_reduce(neg_max[:], chunk_max[:].rearrange("p a j c -> p (a j) c"), AX.X, ALU.max,
                                          negate=True).then_inc(neg_ok, 1)
                        chain = Counted(dve, steps, after * 2)
                        m = len(MAXIMA)
                        psum = ps_m[m % RING_M][0:2 * K_TILES, 0:P]
                        dve.wait_ge(max_ok, after * N_MAX + m + 1)
                        dve.wait_ge(parts_in, (after + 1) * 48)
                        chain.then(dve.tensor_copy(max_parts[:, 0], psum))
                        dve.tensor_tensor(max_rest[:], psum, max_parts[:, 0], ALU.subtract).then_inc(max_used, 1)
                        dve.wait_ge(max_used, after * N_MAX + m + 1 + RING_M)
                        chain.then(dve.tensor_copy(max_parts[:, 1], max_rest[:]))
                        dve.tensor_tensor(max_parts[:, 2], max_rest[:], max_parts[:, 1], ALU.subtract)\
                            .then_inc(parts_ok, 1)

            def add_halves(head, turn):
                slot = turn % RING_O
                dve.wait_ge(o_taken, head * Q_TILES + turn + 2)
                dve.wait_ge(out_stored[slot], (head * Q_TILES // RING_O + turn // RING_O + 1) * 16
                            if isinstance(head, int) else (head * (Q_TILES // RING_O) + turn // RING_O + 1) * 16)
                dve.tensor_tensor(out[:, slot], even[:, slot], odd[:, slot], ALU.add).then_inc(out_ok, 1)

            def step(head, after, at):
                for k in range(N_STEPS):
                    ended = ends(k, 3)
                    if head is not None and ended and not (ended[1] and is_first(head)):
                        add_halves(head - 1 if ended[1] else head, ended[0])
                    if after is not None:
                        maxima(after, maxima_at(k, head is None))
                if head is not None and after is None:
                    add_halves(head, Q_TILES - 1)

            run(dve, step)

        @block.tensor
        def _(pe):
            pe.sem_inc(ones_ok, 2)
            pe.wait_ge(ready, 1)

            def score(head, at, k, a):
                _, tq, kb = STEPS[k]
                lo, n = left(k), 2 * k + a
                psum = ps_s[n % RING_S]
                if n >= RING_S:
                    pe.wait_ge(prob_ok, head * 2 * N_STEPS + n - RING_S + 1)
                elif not is_first(head):
                    pe.wait_ge(prob_ok, head * 2 * N_STEPS - (n == 0))
                diagonal = kb * P >= tq * GROUP
                last = pe.matmul(psum[:, lo:], ks[at][0:WITH_MAX, a, kb * P:(kb + 1) * P],
                                 qs[at][0:WITH_MAX, a, tq * GROUP + lo:(tq + 1) * GROUP], start=True,
                                 stop=not diagonal)
                if diagonal:
                    last = pe.matmul(psum[:, lo:lo + P], core.ident_bf[:], core.mask_k_bf[:], start=False, stop=True)
                last.then_inc(score_ok, 1)

            def clear(psum):
                pe.matmul(psum[:], zeros[:, 0:P], zeros[:, P:], start=True, stop=False)

            def values(head, at, k):
                turn, tq, kb = STEPS[k]
                pe.wait_ge(prob_ok, head * 2 * N_STEPS + 2 * k + 4)
                if kb == 0:
                    pe.wait_ge(o_taken, head * Q_TILES + turn + 1)
                    if tq == 0:
                        clear(ps_o)
                for n in range(2):
                    for a in range(2):
                        strip, lo = (n * 2 + a) * DV, left(k + n)
                        last = pe.matmul(ps_o[strip:strip + DV, lo:], vh[at][:, kb + n],
                                         probs[:, (k + n) % RING_P, a, lo:], start=tq > 0 and kb == 0,
                                         stop=kb == GT * (tq + 1) - 2, tile_position=(0, strip))
                last.then_inc(values_ok, 2)

            def ones(head, quad):
                turn, tq, kb = STEPS[quad * QUAD]
                pe.wait_ge(pair_ok, head * (N_STEPS // 2) + (quad + 1) * (QUAD // 2))
                if kb == 0:
                    pe.wait_ge(l_taken, head * Q_TILES + turn + 1)
                    if tq == 0:
                        clear(ps_l)
                for pair in range(QUAD // 2):
                    k = quad * QUAD + 2 * pair
                    for a in range(2):
                        strip = (2 * pair + a) * DV
                        last = pe.matmul(ps_l[strip:strip + DV, left(k):], core.c("ones")[:, 0:DV],
                                         probs[:, k % RING_P, a, left(k):], start=tq > 0 and kb == 0,
                                         stop=kb == GT * tq, tile_position=(0, strip))
                last.then_inc(ones_ok, 1)

            def maxima(after, at, items):
                for m in items:
                    a, jq, c = MAXIMA[m]
                    w = width(m)
                    diagonal = c == jq // GT
                    pe.wait_ge(max_used, after * N_MAX + m + 1)
                    last = pe.matmul(ps_m[m % RING_M][:, 0:w], qs[at][0:STACK, a, jq * P:(jq + 1) * P],
                                     ks[at][0:STACK, a, c * GROUP:c * GROUP + w], start=True, stop=not diagonal)
                    if diagonal:
                        last = pe.matmul(ps_m[m % RING_M][:, w - P:w], core.ident_bf[:], core.mask_q_bf[:],
                                         start=False, stop=True)
                    last.then_inc(max_ok, 1)

            def turn_maxima(after):
                m = len(MAXIMA)
                pe.wait_ge(neg_ok, after + 1)
                pe.wait_ge(max_used, after * N_MAX + m + 1)
                pe.transpose(ps_m[m % RING_M][0:2 * K_TILES, 0:P], neg_max[:], core.c("ident")).then_inc(max_ok, 1)

            def step(head, after, at):
                if head is None:
                    pe.wait_ge(loaded[0], LOADS * 16)
                    maxima(0, 0, range(len(MAXIMA)))
                    turn_maxima(0)
                    return
                if is_first(head):
                    pe.wait_ge(parts_in, (head + 2) * 48)
                    for n in range(RING_S):
                        score(head, at, n // 2, n % 2)
                pe.wait_ge(v_ok, head + 1)
                score(head, at, 1, 1)
                for k in range(0, N_STEPS, 2):
                    items = [] if after is None else [*maxima_at(k, False), *maxima_at(k + 1, False)]
                    if after is not None and k == FIRST_MAX:
                        if isinstance(after, int):
                            pe.wait_ge(loaded[1 - at], (after // 2 + 1) * LOADS * 16)
                        else:
                            pe.wait_ge(loaded[1 - at], after * (LOADS * 8) + LOADS * (16 if at == 1 else 8))
                    more = k + 2 < N_STEPS
                    if more:
                        score(head, at, k + 2, 0)
                        score(head, at, k + 2, 1)
                    third = -(-len(items) // 3)
                    maxima(after, 1 - at, items[:third])
                    if more:
                        score(head, at, k + 3, 0)
                    elif after is not None:
                        pe.wait_ge(parts_in, (after + 2) * 48)
                        score(after, 1 - at, 0, 0)
                    values(head, at, k)
                    if not more and after is not None:
                        score(after, 1 - at, 0, 1)
                        score(after, 1 - at, 1, 0)
                    maxima(after, 1 - at, items[third:2 * third])
                    if more:
                        score(head, at, k + 3, 1)
                    maxima(after, 1 - at, items[2 * third:])
                    if k >= QUAD and k % QUAD == 0:
                        ones(head, k // QUAD - 1)
                    elif k == 0 and not is_first(head):
                        ones(head - 1, QUADS - 1)
                    if after is not None and k == TURN_MAX:
                        turn_maxima(after)
                if after is None:
                    ones(head, QUADS - 1)

            run(pe, step)


def attention0_out(nc, core, oT, sums, lambdas, rms_scale, woT):
    with stage(nc, "out0") as s:
        lam_in = s.sb("lam_in", [P, 4, H, DH], F32)
        lam_two = s.sb("lam_two", [P, 2, H], F32)
        lam = s.sb("lam", [P, H], F32)
        w = s.sb("wo0", [P, DQ // P, D], F32)
        scale = s.sb("rms_scale_sb", [P, 1], F32)
        heads = [s.sb(f"heads{i}", [P, 2 * DQ // P, GROUP], F32) for i in range(2)]
        total = [s.sb(f"total{i}", [4 * H, GROUP], F32) for i in range(2)]
        recip = s.sb("recip", [P, GT, H, 2], F32)
        two = s.sb("two", [P, GT, H, 2, DV], F32)
        o = [s.sb(f"o{i}", [P, GT, H, DV], F32) for i in range(2)]
        gate = s.sb("gate", [P, B * NG // 2, D], F32)
        square = s.sb("square", [P, GT, H, DV], F32)
        mean = [s.sb(f"mean_sq{i}", [P, GT, H], F32) for i in range(2)]
        oT_sb = s.sb("oT_sb", [P, 2, DQ // P, P], F32)
        gated = s.sb("gated", [P, 2, D], F32)
        ps_h = [s.ps(f"ps_h{i}", [P, H, 2, DV]) for i in range(2)]
        ps_l = s.ps("ps_l", [P, GT, H, 2])
        ps_t = s.ps("ps_t3", [P, DQ // P, P])
        ps_y = [s.ps(f"ps_y{i}", [P, D]) for i in range(2)]
        names = ("w_in", "lam_prod", "lam_exp", "lam_ok", "w_ok", "recip_ok", "steps", "l_steps", "turned_l", "turned_h",
                 "two_ok", "sub_ok", "square_ok", "mean_ok", "root_ok", "o_ok", "turned_o", "oT_ok", "y_ok", "x_ok")
        (w_in, lam_prod, lam_exp, lam_ok, w_ok, recip_ok, steps, l_steps, turned_l, turned_h, two_ok, sub_ok, square_ok,
         mean_ok, root_ok, o_ok, turned_o, oT_ok, y_ok, x_ok) = (s.sem(n) for n in names)
        loaded = [s.sem(f"loaded{i}") for i in range(2)]
        block = s.engines()
        ROWS = 2 * DQ // P

        def run(engine, step):
            last = B * NG // 2 - 1
            step(None, 0, 1, -1)
            with engine.Fori(0, last) as i:
                step(2 * i, 2 * i + 1, 0, i)
                step(2 * i + 1, 2 * i + 2, 1, i)
            step(2 * last, 2 * last + 1, 0, last)
            step(2 * last + 1, None, 1, last)

        @block.sync
        def _(sp):
            for n, a in enumerate(lambdas):
                sp.dma_start(lam_in[:, n], a.rearrange("h d -> (h d)").partition_broadcast(P)
                             .rearrange("p (h d) -> p h d", h=H)).then_inc(w_in, 16)
            sp.dma_start(w[:], woT.rearrange("(k p) n -> p k n", p=P)).then_inc(w_in, 16)
            for strip in range(P // DV):
                sp.dma_start(scale[strip * DV:(strip + 1) * DV], rms_scale.rearrange("(d a) -> d a", a=1))\
                    .then_inc(w_in, 16)

            def step(b, g, i, at):
                start = sp.snap(i * 2 * GROUP + at * GROUP)
                wait_apart(sp, turned_h, g * GT + 1, core.passed)
                sp.dma_start(heads[at][:], oT[b * H:(b + 1) * H, :, ds(start, GROUP)].rearrange(
                    "(r n) e t -> (n e) r t", n=2)).then_inc(loaded[at], 16)
                sp.dma_start(total[at][:], sums[b * H:(b + 1) * H, :, ds(start, GROUP)].rearrange(
                    "n e t -> (n e) t")).then_inc(loaded[at], 16)

            for b in range(B):
                with sp.Fori(0, NG // 2) as i:
                    for at in range(2):
                        step(b, i * 2 + (b * NG + at), i, at)
            sp.wait_ge(loaded[0], B * NG * 16)
            sp.wait_ge(loaded[1], B * NG * 16)

        @block.scalar
        def _(act):
            act.wait_ge(lam_prod, 1)
            act.activation(lam_two[:], lam_two[:], ACT.Exp).then_inc(lam_exp, 1)

            def step(now, after, at, pair):
                if now is None:
                    return
                act.wait_ge(mean_ok, now + 1)
                act.activation(mean[at][:], mean[at][:], ACT.Sqrt).then_inc(root_ok, 1)
                for j in range(GT):
                    act.wait_ge(y_ok, now * GT + j + 1)
                    act.wait_ge(turned_o, now * GT + j + 1)
                    act.activation(oT_sb[:, j % 2], ps_t[:], ACT.Copy).then_inc(oT_ok, 1)

            run(act, step)

        @block.gpsimd
        def _(pool):
            def step(now, after, at, pair):
                if after is None:
                    return
                for j in range(GT):
                    pool.wait_ge(two_ok, after * GT + j + 3)
                    pool.tensor_tensor(o[1 - at][:, j], two[:, j, :, 0], two[:, j, :, 1], ALU.subtract)\
                        .then_inc(sub_ok, 1)
                    pool.wait_ge(sub_ok, after * GT + j + 1)
                    pool.tensor_tensor(square[:, j], o[1 - at][:, j], o[1 - at][:, j], ALU.mult).then_inc(square_ok, 1)

            run(pool, step)

        @block.vector
        def _(dve):
            chain = Counted(dve, lam_ok)
            dve.wait_ge(w_in, 16 * 9)
            chain.then(dve.tensor_tensor(lam_in[:, 0], lam_in[:, 0], lam_in[:, 1], ALU.mult))
            chain.then(dve.tensor_tensor(lam_in[:, 2], lam_in[:, 2], lam_in[:, 3], ALU.mult))
            dve.tensor_reduce(lam_two[:, 0], lam_in[:, 0], AX.X, ALU.add)
            dve.tensor_reduce(lam_two[:, 1], lam_in[:, 2], AX.X, ALU.add).then_inc(lam_prod, 1)
            dve.wait_ge(lam_exp, 1)
            chain.then(dve.tensor_tensor(lam[:], lam_two[:, 0], lam_two[:, 1], ALU.subtract))
            chain.then(dve.tensor_scalar(lam[:], lam[:], LAMBDA_INIT, None, ALU.add))
            dve.tensor_scalar(w[:].rearrange("p k n -> p (k n)"), w[:].rearrange("p k n -> p (k n)"), scale[:, 0:1],
                              1.0 - LAMBDA_INIT, ALU.mult, ALU.mult).then_inc(w_ok, 1)

            for pair in range(B * NG // 2):
                chain.then(dve.tensor_copy(gate[:, pair], core.rows[:, 0, pair // (NG // 2), GATE_A]))
            dve.sem_inc(two_ok, 2)
            dve.sem_inc(x_ok, 4)

            def squares_of(after, j, at):
                dve.wait_ge(square_ok, after * GT + j + 1)
                dve.tensor_reduce(mean[at][:, j], square[:, j], AX.X, ALU.add).then_inc(steps, 1)

            def norm(now, at):
                dve.wait_ge(steps, (now + 1) * GT)
                dve.tensor_scalar(mean[at][:], mean[at][:], 1.0 / DV, LN_EPS, ALU.mult, ALU.add).then_inc(mean_ok, 1)
                dve.wait_ge(root_ok, now + 1)
                dve.reciprocal(mean[at][:], mean[at][:]).then_inc(recip_ok, 1)
                dve.wait_ge(recip_ok, now + 1)
                for j in range(GT):
                    dve.tensor_tensor(o[at][:, j], o[at][:, j], mean[at][:, j].unsqueeze(2)
                                      .broadcast_to([P, H, DV]), ALU.mult).then_inc(o_ok, 1)

            def invert_totals(after):
                dve.wait_ge(turned_l, after + 1)
                dve.reciprocal(recip[:], ps_l[:]).then_inc(l_steps, 1)
                dve.wait_ge(l_steps, 2 * after + 1)
                dve.tensor_tensor(recip[:, :, :, 1], recip[:, :, :, 1],
                                  lam[:].unsqueeze(1).broadcast_to([P, GT, H]), ALU.mult).then_inc(l_steps, 1)
                dve.wait_ge(l_steps, 2 * after + 2)

            def normalise(after, j):
                dve.wait_ge(turned_h, after * GT + j + 2 + GT)
                dve.tensor_tensor(two[:, j].rearrange("p h a d -> p (h a) d"),
                                  ps_h[j % 2][:].rearrange("p h a d -> p (h a) d"),
                                  recip[:, j].rearrange("p h a -> p (h a)").unsqueeze(2)
                                  .broadcast_to([P, 2 * H, DV]), ALU.mult).then_inc(two_ok, 1)

            def add(now, j, pair):
                t = now * GT + j
                dve.wait_ge(y_ok, t + 3)
                dve.tensor_tensor(gated[:, j % 2].unsqueeze(1), ps_y[j % 2][:].unsqueeze(1),
                                  gate[:, ds(pair, 1), :], ALU.mult).then_inc(x_ok, 1)
                dve.wait_ge(x_ok, t * 2 + 5)
                dve.tensor_tensor(core.x[:, ds(t, 1), :], core.x[:, ds(t, 1), :], gated[:, j % 2:j % 2 + 1],
                                  ALU.add).then_inc(x_ok, 1)

            def step(now, after, at, pair):
                if now is not None:
                    norm(now, at)
                if after is not None:
                    invert_totals(after)
                    normalise(after, 0)
                for j in range(GT):
                    if after is not None and j + 1 < GT:
                        normalise(after, j + 1)
                    if now is not None:
                        add(now, j, pair)
                    if after is not None:
                        squares_of(after, j, 1 - at)

            run(dve, step)
            dve.wait_ge(x_ok, B * NG * GT * 2 + 4)

        @block.tensor
        def _(pe):
            pe.sem_inc(turned_h, GT + 1)
            pe.wait_ge(w_ok, 1)

            pe.sem_inc(y_ok, 2)

            def turn_totals(after, place, pair):
                wait_apart(pe, loaded[place], pair * 32 + 32, core.passed)
                for j in range(GT):
                    last = pe.matmul(ps_l[:, j].rearrange("p h a -> p (h a)"), total[place][:, j * P:(j + 1) * P],
                                     core.c("fold")[0:4 * H], start=True, stop=True)
                last.then_inc(turned_l, 1)

            def turn(after, place, j):
                pe.wait_ge(two_ok, after * GT + j + 1)
                for r in range(ROWS):
                    last = pe.transpose(ps_h[j % 2][:, 2 * r:2 * r + 2].rearrange("p h a d -> p (h a d)"),
                                        heads[place][:, r, j * P:(j + 1) * P], core.c("ident"))
                last.then_inc(turned_h, 1)

            def turn_back(now, j, at):
                pe.wait_ge(o_ok, now * GT + j + 1)
                for k in range(DQ // P):
                    last = pe.transpose(ps_t[:, k], o[at][:, j, 4 * k:4 * k + 4].rearrange("p h d -> p (h d)"),
                                        core.c("ident"))
                last.then_inc(turned_o, 1)

            def step(now, after, at, pair):
                if after is not None:
                    turn_totals(after, 1 - at, pair + at)
                    turn(after, 1 - at, 0)
                    turn(after, 1 - at, 1)
                if now is not None:
                    turn_back(now, 0, at)
                for j in range(GT):
                    if after is not None and j + 2 < GT:
                        turn(after, 1 - at, j + 2)
                    if now is None:
                        continue
                    pe.wait_ge(oT_ok, now * GT + j + 1)
                    if j + 1 < GT:
                        turn_back(now, j + 1, at)
                    pe.wait_ge(x_ok, (now * GT + j) * 2 + 2)
                    for k in range(DQ // P):
                        last = pe.matmul(ps_y[j % 2][:], oT_sb[:, j % 2, k], w[:, k], start=(k == 0),
                                         stop=(k == DQ // P - 1))
                    last.then_inc(y_ok, 1)

            run(pe, step)


def gates(nc, core, layer, wg, h_rows, scores):
    with stage(nc, f"gates{layer}") as s:
        w = s.sb("wg_sb", [P, DC, NE], F32)
        stats = s.sb("stats", [P, GT, 6], F32)
        mv = s.sb("mean_var", [P, GT, 2], F32)
        rstd = s.sb("rstd", [P, GT], F32)
        scaled = s.sb("scaled", [P, GT, D], F32)
        h = [s.sb(f"h{i}", [P, GT, D], F32) for i in range(2)]
        hT = s.sb("hT", [P, DC, GROUP], F32)
        most = s.sb("most", [P, T], F32)
        ps_t = [s.ps(f"ps_t{i}", [P, DC, GROUP]) for i in range(2)]
        ps_g = s.ps("ps_g", [P, T, NE])
        names = ("w_in", "steps", "var_ok", "std_ok", "h_ok", "turned", "hT_ok", "logits_ok", "soft", "exp_ok",
                 "scores_out")
        (w_in, steps, var_ok, std_ok, h_ok, turned, hT_ok, logits_ok, soft, exp_ok,
         scores_out) = (s.sem(n) for n in names)
        stored = [s.sem(f"stored{i}") for i in range(2)]
        block = s.engines()
        h_view = h_rows.rearrange("(t p) c -> p t c", p=P)
        LINKS = NORM_LINKS + 1

        def run(engine, step):
            for b in range(B):
                with engine.Fori(0, NG // 2) as i:
                    for at in range(2):
                        step(b, i * 2 + (b * NG + at), at)

        @block.sync
        def _(sp):
            sp.dma_start(w[:], wg.rearrange("(k p) n -> p k n", p=P)).then_inc(w_in, 16)
            sp.wait_ge(w_in, 16)
            for at in range(2):
                sp.sem_inc(stored[at], 16)

            def step(b, g, at):
                tile = sp.snap(g * GT)
                wait_apart(sp, h_ok, g + 2, core.passed)
                sp.dma_start(h_view[:, ds(tile, GT), 0:D], h[at][:]).then_inc(stored[at], 16)

            run(sp, step)
            for at in range(2):
                sp.wait_ge(stored[at], (B * NG // 2 + 1) * 16)
            if h_rows.shape[1] > D:
                sp.wait_ge(soft, 4)
                with nc.allow_non_contiguous_dma(reason="eight scores of a row"):
                    sp.dma_start(h_view[:, :, D:], scores[:]).then_inc(scores_out, 16)
                sp.wait_ge(scores_out, 16)

        @block.scalar
        def _(act):
            act.sem_inc(hT_ok, 2)

            def root(g):
                act.wait_ge(var_ok, g + 1)
                act.activation(rstd[:], mv[:, :, 1], ACT.Sqrt).then_inc(std_ok, 1)

            def copy(g, at):
                act.wait_ge(logits_ok, g + 1)
                act.wait_ge(turned, g + 3)
                act.activation(hT[:], ps_t[at][:], ACT.Copy).then_inc(hT_ok, 1)

            root(0)
            with act.Fori(0, B * NG // 2 - 1) as i:
                for at in range(2):
                    root(2 * i + (at + 1))
                    copy(2 * i + at, at)
            root(B * NG - 1)
            copy(B * NG - 2, 0)
            copy(B * NG - 1, 1)
            act.wait_ge(soft, 1)
            act.activation(scores[:], scores[:], ACT.Exp).then_inc(exp_ok, 1)

        @block.vector
        def _(dve):
            dve.sem_inc(h_ok, 1)

            def step(b, g, at):
                chain = Counted(dve, steps, g * LINKS)
                wait_apart(dve, h_ok, g + 1, core.passed)
                norm_statistics(dve, chain, core, g, mv, stats, rstd, var_ok, std_ok)
                for j in range(GT):
                    last = dve.scalar_tensor_tensor(scaled[:, j], core.x[:, ds(g * GT + j, 1), :].rearrange(
                        "p a d -> p (a d)"), mv[:, j, 0:1], core.rows[:, layer, b, SCALE_B], ALU.subtract, ALU.mult)
                chain.then(last)
                dve.wait_ge(stored[at], (g * 8 + (16 - 8 * at)))
                dve.wait_ge(turned, g + 1)
                for j in range(GT):
                    last = dve.scalar_tensor_tensor(h[at][:, j], scaled[:, j], rstd[:, j:j + 1],
                                                    core.rows[:, layer, b, SHIFT_B], ALU.mult, ALU.add)
                last.then_inc(h_ok, 1)

            run(dve, step)
            dve.wait_ge(logits_ok, B * NG + 1)
            chain = Counted(dve, steps, B * NG * LINKS)
            chain.then(dve.tensor_reduce(most[:], ps_g[:], AX.X, ALU.max))
            wide = most[:].unsqueeze(2).broadcast_to([P, T, NE])
            dve.tensor_tensor(scores[:], ps_g[:], wide, ALU.subtract).then_inc(soft, 1)
            dve.wait_ge(exp_ok, 1)
            dve.tensor_reduce(most[:], scores[:], AX.X, ALU.add).then_inc(soft, 1)
            dve.wait_ge(soft, 2)
            dve.reciprocal(most[:], most[:]).then_inc(soft, 1)
            dve.wait_ge(soft, 3)
            dve.tensor_tensor(scores[:], scores[:], wide, ALU.mult).then_inc(soft, 1)

        @block.tensor
        def _(pe):
            pe.wait_ge(w_in, 16)
            pe.sem_inc(turned, 2)
            pe.sem_inc(logits_ok, 1)

            def step(b, g, at):
                pe.wait_ge(h_ok, g + 2)
                pe.wait_ge(hT_ok, g + 1)
                for k in range(DC):
                    for j in range(GT):
                        last = pe.transpose(ps_t[at][:, k, j * P:(j + 1) * P], h[at][:, j, k * P:(k + 1) * P],
                                            core.c("ident"))
                last.then_inc(turned, 1)
                pe.wait_ge(hT_ok, g + 3)
                for j in range(GT):
                    for k in range(DC):
                        last = pe.matmul(ps_g[:, ds(g * GT + j, 1)], hT[:, k, j * P:(j + 1) * P], w[:, k],
                                         start=(k == 0), stop=(k == DC - 1))
                last.then_inc(logits_ok, 1)

            run(pe, step)




def prefix(dve, pe_done, chain, mask, ps_in, ps_all, sums, out):
    dve.wait_ge(*pe_done)
    chain.then(dve.tensor_copy(sums[0][:], ps_all[:]))
    now, width = 0, 1
    while width < T:
        a, b = sums[now], sums[1 - now]
        dve.tensor_copy(b[:, 0:width], a[:, 0:width])
        chain.then(dve.tensor_tensor(b[:, width:], a[:, width:], a[:, 0:T - width], ALU.add))
        now, width = 1 - now, 2 * width
    totals, spare = sums[now], sums[1 - now]
    chain.then(dve.tensor_tensor(spare[:], totals[:], ps_all[:], ALU.subtract))
    chain.then(dve.tensor_tensor(out[:], spare[:], ps_in[:], ALU.add))
    return totals


def listing0(nc, core, place, slots):
    chunks = CAP0 // P
    with stage(nc, "list0") as s:
        place_i = s.sb("place_i", [P, T, NE], I32)
        low_i = s.sb("low_i", [P, T, NE], I32)
        low = s.sb("low", [P, T, NE], BF16)
        iota = s.sb("iota", [P, P], BF16)
        high = s.sb("high", [P, T, NE], F32)
        hot = s.sb("hot", [P, T * NE, chunks], F32)
        marks = s.sb("marks", [P, T, NE, 2, chunks], BF16)
        hot_low = [s.sb(f"hot_low{i}", [P, NE, P], BF16) for i in range(2)]
        zeros = s.sb("zeros", [P, P], BF16)
        tokens = s.sb("tokens", [P, NE, chunks], F32)
        ps = s.ps("ps_list", [P, NE, 2, chunks])
        steps, marks_ok, zero_ok, low_ok, low_used, done = (s.sem(n) for n in (
            "steps", "marks_ok", "zero_ok", "low_ok", "low_used", "done"))
        block = s.engines()

        @block.vector
        def _(dve):
            chain = Counted(dve, steps)
            dve.memset(zeros[:], 0.0).then_inc(zero_ok, 1)
            dve.tensor_copy(iota[:], core.c("iota"))
            chain.then(dve.tensor_copy(place_i[:], place[:]))
            dve.tensor_single_scalar(low_i[:], place_i[:], P - 1, ALU.bitwise_and)
            chain.then(dve.tensor_single_scalar(place_i[:], place_i[:], 7, ALU.arith_shift_right))
            dve.tensor_copy(low[:], low_i[:])
            chain.then(dve.tensor_copy(high[:], place_i[:]))
            chain.then(dve.tensor_tensor(hot[:], high[:].rearrange("p t e -> p (t e)").unsqueeze(2)
                                         .broadcast_to([P, T * NE, chunks]),
                                         core.c("iota")[:, 0:chunks].unsqueeze(1).broadcast_to([P, T * NE, chunks]),
                                         ALU.is_equal))
            flat = marks[:].rearrange("p t e w c -> p (t e) w c")
            dve.tensor_scalar(flat[:, :, 0], hot[:], core.c("part"), None, ALU.mult)
            dve.tensor_tensor(flat[:, :, 1], hot[:], core.c("tile_of").unsqueeze(2)
                              .broadcast_to([P, T * NE, chunks]), ALU.mult).then_inc(marks_ok, 1)
            with dve.Fori(0, T // 2) as i:
                for at in range(2):
                    dve.wait_ge(low_used, i * 2 + (at + 1))
                    dve.tensor_tensor(hot_low[at][:].rearrange("p e (a r) -> p a e r", a=1),
                                      low[:, ds(i * 2 + at, 1), :].unsqueeze(3).broadcast_to([P, 1, NE, P]),
                                      iota[:].unsqueeze(1).unsqueeze(1).broadcast_to([P, 1, NE, P]),
                                      ALU.is_equal).then_inc(low_ok, 1)
            dve.wait_ge(low_used, T + 2)
            chain.then(dve.tensor_scalar(tokens[:], ps[:, :, 1], float(P), None, ALU.mult))
            chain.then(dve.tensor_tensor(slots[:], tokens[:], ps[:, :, 0], ALU.add))

        @block.tensor
        def _(pe):
            pe.sem_inc(low_used, 2)
            pe.wait_ge(zero_ok, 1)
            pe.wait_ge(marks_ok, 1)
            pe.matmul(ps[:].rearrange("p e w c -> p (e w c)"), zeros[:],
                      marks[:, 0].rearrange("p e w c -> p (e w c)"), start=True, stop=False, skip_group_check=True)
            with pe.Fori(0, T // 2) as i:
                for at in range(2):
                    pe.wait_ge(low_ok, i * 2 + (at + 1))
                    for e in range(NE):
                        last = pe.matmul(ps[:, e].rearrange("p w c -> p (w c)"), hot_low[at][:, e],
                                         marks[:, ds(i * 2 + at, 1), e].rearrange("p t w c -> p (t w c)"),
                                         start=False, stop=False, skip_group_check=True)
                    last.then_inc(low_used, 1)


def route0(nc, core, scores, place):
    TOP_BIT = 29
    ROUNDS = (TOP_BIT + 1) // 2
    with stage(nc, "route0") as s:
        level = s.sb("level", [P, NE], I32)
        trial = s.sb("trial", [P, 3, NE], I32)
        bits = s.sb("bits", [P, 3, NE], I32)
        reached = s.sb("reached", [P, 3, NE], F32)
        add = s.sb("add", [P, NE], I32)
        tried = s.sb("tried", [P, 3, T, NE], F32)
        counts = s.sb("counts", [P, 3, NE], F32)
        above = s.sb("above", [P, T, NE], F32)
        equal = s.sb("equal", [P, T, NE], F32)
        count = s.sb("count", [P, NE], F32)
        room = s.sb("room", [P, NE], F32)
        sums = [s.sb(f"sums{i}", [P, T, NE], F32) for i in range(2)]
        rank = s.sb("rank", [P, T, NE], F32)
        ps_c = s.ps("ps_c", [P, NE])
        ps_3 = s.ps("ps_3", [P, 3, NE])
        ps_in = s.ps("ps_in", [P, T, NE])
        ps_all = s.ps("ps_all", [P, T, NE])
        steps, count_ok, total_ok, mask_ok, sums_ok = (s.sem(n) for n in (
            "steps", "count_ok", "total_ok", "mask_ok", "sums_ok"))
        block = s.engines()

        def at_least(dve, out, bits, op):
            return dve.tensor_tensor(out[:], scores[:], bits[:].bitcast(F32).unsqueeze(1)
                                     .broadcast_to([P, T, NE]), op)

        @block.vector
        def _(dve):
            chain = Counted(dve, steps)
            dve.memset(level[:], 0)
            for n in range(3):
                last = dve.memset(bits[:, n], (n + 1) << (TOP_BIT - 1))
            chain.then(last)
            before, PER = chain.n, 4
            with dve.Fori(0, ROUNDS) as i:
                chain = Counted(dve, steps, i * PER + before)
                chain.then(dve.tensor_tensor(trial[:], level[:].unsqueeze(1).broadcast_to([P, 3, NE]), bits[:],
                                             ALU.bitwise_or))
                chain.then(dve.tensor_tensor(tried[:], scores[:].unsqueeze(1).broadcast_to([P, 3, T, NE]),
                                             trial[:].bitcast(F32).unsqueeze(2).broadcast_to([P, 3, T, NE]),
                                             ALU.is_ge))
                dve.tensor_reduce(counts[:], tried[:].rearrange("p n t e -> p n e t"), AX.X, ALU.add)\
                    .then_inc(count_ok, 1)
                dve.wait_ge(total_ok, i + 1)
                chain.then(dve.scalar_tensor_tensor(reached[:], ps_3[:], float(CAP0), bits[:], ALU.is_ge, ALU.mult))
                dve.tensor_reduce(add[:], reached[:].rearrange("p n e -> p e n"), AX.X, ALU.max)
                chain.then(dve.tensor_single_scalar(bits[:], bits[:], 2, ALU.arith_shift_right))
                assert chain.n == PER
                dve.tensor_tensor(level[:], level[:], add[:], ALU.bitwise_or).then_inc(mask_ok, 1)
                dve.wait_ge(mask_ok, i + 1)
            chain = Counted(dve, steps, before + ROUNDS * PER)
            at_least(dve, above, level, ALU.is_gt)
            chain.then(at_least(dve, equal, level, ALU.is_equal))
            dve.tensor_reduce(count[:], above[:].rearrange("p t e -> p e t"), AX.X, ALU.add).then_inc(mask_ok, 1)
            dve.wait_ge(sums_ok, 1)
            chain.then(dve.tensor_scalar(room[:], ps_c[:], -1.0, float(CAP0), ALU.mult, ALU.add))
            prefix(dve, (sums_ok, 1), chain, equal, ps_in, ps_all, sums, rank)
            wide = room[:].unsqueeze(1).broadcast_to([P, T, NE])
            chain.then(dve.tensor_tensor(rank[:], rank[:], wide, ALU.is_lt))
            chain.then(dve.tensor_tensor(equal[:], equal[:], rank[:], ALU.mult))
            dve.tensor_tensor(above[:], above[:], equal[:], ALU.add).then_inc(mask_ok, 1)
            prefix(dve, (sums_ok, 2), chain, above, ps_in, ps_all, sums, place)
            chain.then(dve.tensor_scalar(equal[:], above[:], -8192.0, 8192.0, ALU.mult, ALU.add))
            chain.then(dve.tensor_tensor(place[:], place[:], equal[:], ALU.add))

        @block.tensor
        def _(pe):
            with pe.Fori(0, ROUNDS) as i:
                pe.wait_ge(count_ok, i + 1)
                pe.matmul(ps_3[:].rearrange("p n e -> p (n e)"), core.c("ones"),
                          counts[:].rearrange("p n e -> p (n e)"), start=True, stop=True).then_inc(total_ok, 1)

            def prefixes(mask):
                flat = mask[:].rearrange("p t e -> p (t e)")
                pe.matmul(ps_in[:].rearrange("p t e -> p (t e)"), core.c("before"), flat, start=True, stop=True)
                pe.matmul(ps_all[:].rearrange("p t e -> p (t e)"), core.c("ones"), flat, start=True, stop=True)\
                    .then_inc(sums_ok, 1)

            pe.wait_ge(mask_ok, ROUNDS + 1)
            pe.matmul(ps_c[:], core.c("ones"), count[:], start=True, stop=True)
            prefixes(equal)
            pe.wait_ge(mask_ok, ROUNDS + 2)
            prefixes(above)


class Unit:

    def __init__(self, pair, n, per):
        if isinstance(pair, int):
            pair, n = pair + n // (2 * per), n % (2 * per)
        self.pair = pair + 1 if n >= 2 * per else pair
        self.u = pair * (2 * per) + n
        self.e = pair * 2 + n // per
        self.part, self.at = n % per, n // per % 2


def unit_steps(engine, per, step, ahead=1):
    for n in range(ahead):
        step(None, Unit(0, n, per))
    with engine.Fori(0, NE // 2 - 1) as i:
        for n in range(2 * per):
            step(Unit(i, n, per), Unit(i, n + ahead, per))
    for n in range(2 * per):
        step(Unit(NE // 2 - 1, n, per), Unit(NE // 2 - 1, n + ahead, per) if n + ahead < 2 * per else None)


def experts0(nc, core, h_rows, slots, w1, w3, w2, added):
    CH = CAP0 // P
    UC = GT
    MC = HID0 // P
    UNITS = 2 * NE
    with stage(nc, "experts0") as s:
        w_up = [[s.sb(f"w{n}_{i}", [P, DC, HID0], F32) for i in range(2)] for n in (1, 3)]
        w_down = [s.sb(f"w2_{i}", [P, MC, D], F32) for i in range(2)]
        index = [s.sb(f"index{i}", [P, CH], I32) for i in range(2)]
        rows = [s.sb(f"gathered{i}", [P, UC, D + NE], F32) for i in range(2)]
        score = [s.sb(f"score{i}", [P, UC, 1], F32) for i in range(2)]
        scaled = s.sb("scaled", [P, UC, D], F32)
        xT = [s.sb(f"xT{i}", [P, DC, GROUP], F32) for i in range(2)]
        silu = s.sb("silu", [P, 2, GROUP], F32)
        hT = s.sb("hidT", [P, MC, GROUP], F32)
        out = [s.sb(f"y_sb{i}", [P, UC, D], F32) for i in range(2)]
        zeros = s.sb("zeros", [P, 4, D], F32)
        ps_t = s.ps("ps_t", [P, DC, GROUP])
        ps_a = [s.ps(f"ps_a{i}", [P, GROUP]) for i in range(2)]
        ps_b = [s.ps(f"ps_b{i}", [P, GROUP]) for i in range(2)]
        ps_y = [s.ps(f"ps_y{i}", [P, 2, D]) for i in range(2)]
        names = ("zero_ok", "zero_out", "index_ok", "score_ok", "scaled_ok", "turned", "xT_ok", "up_ok",
                 "silu_ok", "hid_ok", "down_ok", "out_ok", "out_free", "scattered")
        (zero_ok, zero_out, index_ok, score_ok, scaled_ok, turned, xT_ok, up_ok, silu_ok, hid_ok, down_ok,
         out_ok, out_free, scattered) = (s.sem(n) for n in names)
        w_in = [s.sem(f"w_in{i}") for i in range(2)]
        gathered = [s.sem(f"gathered{i}") for i in range(2)]
        block = s.engines()

        @block.sync
        def _(sp):
            def load(e, at):
                for to, w in ((w_up[0], w1), (w_up[1], w3), (w_down, w2)):
                    sp.dma_start(to[at][:], w[ds(e, 1)].rearrange("e (k p) n -> p (e k) n", p=P)).then_inc(
                        w_in[at], 16)

            load(0, 0)
            load(1, 1)
            sp.wait_ge(zero_ok, 1)
            for n in range(T // 4):
                sp.dma_start(added.rearrange("(t p) d -> p t d", p=P)[:, 4 * n:4 * n + 4], zeros[:]).then_inc(
                    zero_out, 16)
            with sp.Fori(0, NE // 2 - 1) as i:
                for at in range(2):
                    e = sp.snap(2 * i + (at + 2))
                    wait_apart(sp, down_ok, 8 * i + 4 * (at + 1), core.passed)
                    load(e, at)

        @block.gpsimd
        def _(pool):
            pool.sem_inc(out_free, 2)

            def step(now, after):
                if after is not None:
                    if after.part == 0:
                        pool.tensor_copy(index[after.at][:], slots[:, ds(after.e * CH, CH)]).then_inc(index_ok, 1)
                        wait_apart(pool, index_ok, after.e + 1, core.passed)
                    wait_apart(pool, scaled_ok, after.u + 1, core.passed)
                    for c in range(UC):
                        col = after.part * UC + c
                        pool.indirect_dma_start(
                            rows[after.part][:, c], None, h_rows,
                            bass.IndirectOffsetOnAxis(ap=index[after.at][:, col:col + 1], axis=0))\
                            .then_inc(gathered[after.part], 16)
                    if now is None and after.u == 1:
                        pool.wait_ge(zero_out, 16 * T // 4)
                if now is not None:
                    wait_apart(pool, out_ok, (now.u + 2) * 2, core.passed)
                    for c in range(UC):
                        col = now.part * UC + c
                        pool.indirect_dma_start(
                            added, bass.IndirectOffsetOnAxis(ap=index[now.at][:, col:col + 1], axis=0),
                            out[now.part][:, c], None, compute_op=ALU.add).then_inc(scattered, 16)
                    pool.wait_ge(scattered, (now.u + 1) * UC * 16)
                    pool.sem_inc(out_free, 1)

            unit_steps(pool, 2, step, ahead=2)

        @block.scalar
        def _(act):
            act.sem_inc(out_ok, 2)

            def step(now, after):
                if now is not None:
                    for m in range(MC):
                        act.wait_ge(up_ok, now.u * MC + m + 1)
                        act.activation(silu[:, m % 2], ps_a[m % 2][:], ACT.Silu).then_inc(silu_ok, 1)
                if after is not None:
                    act.wait_ge(turned, after.u + 2)
                    act.activation(xT[after.part][:], ps_t[:], ACT.Copy).then_inc(xT_ok, 1)
                if now is not None:
                    act.wait_ge(out_free, now.u + 1)
                    for n in range(2):
                        act.wait_ge(down_ok, now.u * 2 + n + 1)
                        act.activation(out[now.part][:, 2 * n:2 * n + 2], ps_y[n][:], ACT.Copy).then_inc(out_ok, 1)

            unit_steps(act, 2, step)

        @block.vector
        def _(dve):
            dve.memset(zeros[:], 0.0).then_inc(zero_ok, 1)
            dve.sem_inc(scaled_ok, 2)
            dve.sem_inc(hid_ok, 2)

            def step(now, after):
                if after is not None:
                    dve.wait_ge(gathered[after.part], (after.e + 1) * UC * 16)
                    dve.tensor_copy(score[after.part][:], rows[after.part][:, :, ds(after.e + D, 1)]).then_inc(score_ok, 1)
                    dve.wait_ge(score_ok, after.u + 1)
                    dve.wait_ge(turned, after.u + 1)
                    for c in range(UC):
                        last = dve.tensor_scalar(scaled[:, c], rows[after.part][:, c, 0:D],
                                                 score[after.part][:, c], None,
                                                 ALU.mult)
                    last.then_inc(scaled_ok, 1)
                if now is not None:
                    for m in range(MC):
                        dve.wait_ge(silu_ok, now.u * MC + m + 1)
                        dve.tensor_tensor(hT[:, m], ps_b[m % 2][:], silu[:, m % 2], ALU.mult).then_inc(hid_ok, 1)

            unit_steps(dve, 2, step)

        @block.tensor
        def _(pe):
            pe.sem_inc(turned, 1)

            def step(now, after):
                if now is not None:
                    pe.wait_ge(xT_ok, now.u + 1)
                    if now.part == 0:
                        wait_apart(pe, w_in[now.at], now.pair * 48 + 48, core.passed)
                    for m in range(MC):
                        pe.wait_ge(hid_ok, now.u * MC + m + 1)
                        for n, psum in enumerate((ps_a[m % 2], ps_b[m % 2])):
                            for k in range(DC):
                                last = pe.matmul(psum[:], w_up[n][now.at][:, k, m * P:(m + 1) * P],
                                                 xT[now.part][:, k], start=(k == 0), stop=(k == DC - 1))
                        last.then_inc(up_ok, 1)
                if after is not None:
                    pe.wait_ge(scaled_ok, after.u + 3)
                    for k in range(DC):
                        for j in range(UC):
                            last = pe.transpose(ps_t[:, k, j * P:(j + 1) * P], scaled[:, j, k * P:(k + 1) * P],
                                                core.c("ident"))
                    last.then_inc(turned, 1)
                if now is not None:
                    pe.wait_ge(hid_ok, (now.u + 1) * MC + 2)
                    for n in range(2):
                        pe.wait_ge(out_ok, now.u * 2 + n + 1)
                        for c in range(2):
                            for m in range(MC):
                                last = pe.matmul(ps_y[n][:, c], hT[:, m, (2 * n + c) * P:(2 * n + c + 1) * P],
                                                 w_down[now.at][:, m], start=(m == 0), stop=(m == MC - 1))
                        last.then_inc(down_ok, 1)

            unit_steps(pe, 2, step)


def project1(nc, core, added, wq, wk, wv, bq, bk, bv, qT, kT, v):
    with stage(nc, "project1") as s:
        w = s.sb("w", [P, 3, DC, D], F32)
        bias = s.sb("bias", [P, 2, DC], F32)
        bias_v = s.sb("bias_v", [P, D], F32)
        extra = s.sb("extra", [P, GT, D], F32)
        stats = s.sb("stats", [P, GT, 6], F32)
        mv = s.sb("mean_var", [P, GT, 2], F32)
        rstd = s.sb("rstd", [P, GT], F32)
        normed = s.sb("normed", [P, GT, D], F32)
        hT = s.sb("hT", [P, DC, GROUP], F32)
        low = s.sb("low", [P, 2 * DC, GROUP], F32)
        high = s.sb("high", [P, 2 * DC, GROUP], F32)
        ps_t = s.ps("ps_t", [P, DC, GROUP])
        QK = 2 * DC
        VO = GT // 2
        ps_o = [s.ps(f"ps_o{i}", [P, GROUP]) for i in range(QK + VO)]
        names = ("w_in", "steps", "var_ok", "std_ok", "gated_ok", "normed_ok", "turned", "hT_ok", "out_ok",
                 "split_ok", "exp_ok", "sum_ok", "v_ok")
        (w_in, steps, var_ok, std_ok, gated_ok, normed_ok, turned, hT_ok, out_ok, split_ok, exp_ok, sum_ok,
         v_ok) = (s.sem(n) for n in names)
        extra_in = s.sem("extra_in")
        block = s.engines()

        @block.sync
        def _(sp):
            def load(g):
                at = sp.snap(g * GT) if not isinstance(g, int) else g * GT
                if not isinstance(g, int) or g > 0:
                    wait_apart(sp, gated_ok, g, core.passed)
                sp.dma_start(extra[:], added.rearrange("(t p) d -> p t d", p=P)[:, ds(at, GT)]).then_inc(extra_in, 16)

            load(0)
            for n, a in enumerate((wq, wk, wv)):
                sp.dma_start(w[:, n], a.rearrange("(k p) n -> p k n", p=P)).then_inc(w_in, 16)
            for n, a in enumerate((bq, bk)):
                with nc.allow_non_contiguous_dma(reason="a bias to partitions"):
                    sp.dma_start(bias[:, n], a.rearrange("(k p) -> p k", p=P)).then_inc(w_in, 16)
            sp.dma_start(bias_v[:], bv.partition_broadcast(P)).then_inc(w_in, 16)
            with sp.Fori(1, B * NG) as g:
                load(g)

        @block.scalar
        def _(act):
            def root(g):
                act.wait_ge(var_ok, g + 1)
                act.activation(rstd[:], mv[:, :, 1], ACT.Sqrt).then_inc(std_ok, 1)

            def modulate(b, g):
                act.wait_ge(turned, g + 1)
                act.wait_ge(out_ok, g * (QK + VO) + 1)
                for k in range(DC):
                    act.activation(hT[:, k], ps_t[:, k], ACT.Identity, scale=core.pre[:, 1, DC + k, b:b + 1],
                                   bias=core.pre[:, 1, k, b:b + 1]).then_inc(hT_ok, 1)

            def step(b, g, next_b, after):
                for o in range(QK):
                    act.wait_ge(split_ok, g * QK + o + 1 + QK)
                    act.activation(low[:, o], low[:, o], ACT.Exp).then_inc(exp_ok, 1)
                    if o == 0 and after is not None:
                        root(after)
                        modulate(next_b, after)

            root(0)
            modulate(0, 0)
            run_ahead(act, step)

        @block.gpsimd
        def _(pool):
            pool.sem_inc(sum_ok, QK)

            def step(b, g, next_b, after):
                for o in range(QK):
                    to = (qT, kT)[o // DC]
                    wait_apart(pool, exp_ok, g * QK + o + 1, core.passed)
                    pool.tensor_tensor(to[:, o % DC, ds(g * GROUP, GROUP)], high[:, o], low[:, o], ALU.add)\
                        .then_inc(sum_ok, 1)

            run_ahead(pool, step)

        @block.vector
        def _(dve):
            dve.sem_inc(split_ok, QK)
            dve.sem_inc(v_ok, VO)
            dve.wait_ge(w_in, 6 * 16)

            def norm(b, g):
                chain = Counted(dve, steps, g * (NORM_LINKS + 1))
                dve.wait_ge(extra_in, (g + 1) * 16)
                chain.then(dve.tensor_tensor(extra[:], extra[:], core.rows[:, 0, b, GATE_B:GATE_B + 1]
                                             .broadcast_to([P, GT, D]), ALU.mult))
                dve.tensor_tensor(core.x[:, ds(g * GT, GT), :], core.x[:, ds(g * GT, GT), :], extra[:], ALU.add)\
                    .then_inc(gated_ok, 1)
                wait_apart(dve, gated_ok, g + 1, core.passed)
                group_norm(dve, chain, core, g, mv, stats, rstd, normed, var_ok, std_ok, None).then_inc(normed_ok, 1)

            def step(b, g, next_b, after):
                for o in range(QK):
                    dve.wait_ge(out_ok, g * (QK + VO) + o + 2)
                    dve.wait_ge(sum_ok, g * QK + o + 1)
                    column = bias[:, o // DC, o % DC:o % DC + 1]
                    dve.tensor_scalar(low[:, o], ps_o[o][:], column, 0.0, ALU.add, ALU.min)
                    dve.tensor_scalar(high[:, o], ps_o[o][:], column, 0.0, ALU.add, ALU.max).then_inc(split_ok, 1)
                    if o == 0 and after is not None:
                        norm(next_b, after)
                for n in range(VO):
                    dve.wait_ge(out_ok, g * (QK + VO) + QK + n + 2)
                    dve.tensor_tensor(v[:, ds(g * GT + 2 * n, 2), :],
                                      ps_o[QK + n][:].rearrange("p (j d) -> p j d", j=2),
                                      bias_v[:].unsqueeze(1).broadcast_to([P, 2, D]), ALU.add).then_inc(v_ok, 1)

            norm(0, 0)
            run_ahead(dve, step)

        @block.tensor
        def _(pe):
            pe.sem_inc(out_ok, 1)
            pe.wait_ge(w_in, 6 * 16)

            def turn(g):
                pe.wait_ge(normed_ok, g + 1)
                for k in range(DC):
                    for j in range(GT):
                        last = pe.transpose(ps_t[:, k, j * P:(j + 1) * P], normed[:, j, k * P:(k + 1) * P],
                                            core.c("ident"))
                last.then_inc(turned, 1)

            def step(b, g, next_b, after):
                pe.wait_ge(hT_ok, (g + 1) * DC)
                for o in range(QK):
                    pe.wait_ge(split_ok, g * QK + o + 1)
                    for k in range(DC):
                        last = pe.matmul(ps_o[o][:], w[:, o // DC, k, (o % DC) * P:(o % DC + 1) * P], hT[:, k],
                                         start=(k == 0), stop=(k == DC - 1))
                    last.then_inc(out_ok, 1)
                for n in range(VO):
                    if after is not None and n == VO - 1:
                        turn(after)
                    pe.wait_ge(v_ok, g * VO + n + 1)
                    for j in range(2):
                        for k in range(DC):
                            t = 2 * n + j
                            last = pe.matmul(ps_o[QK + n][:, j * D:(j + 1) * D], hT[:, k, t * P:(t + 1) * P],
                                             w[:, 2, k], start=(k == 0), stop=(k == DC - 1))
                    last.then_inc(out_ok, 1)

            turn(0)
            run_ahead(pe, step)


def linear1(nc, core, wo, bo, qT, kT, v):
    CHUNKS = N // P
    G4 = H // 4
    HG = DC
    with stage(nc, "linear1") as s:
        w = s.sb("wo", [P, DC, D], F32)
        bias = s.sb("bias", [P, D], F32)
        kc = [s.sb(f"kc{i}", [P, HG, P], F32) for i in range(2)]
        vp = [s.sb(f"vp{i}", [P, H, 32], F32) for i in range(2)]
        qblk = s.sb("qblk", [P, HG, NE, P], F32)
        masked = [s.sb(f"masked{i}", [P, HG, NE, P], F32) for i in range(2)]
        k_tok = [s.sb(f"k_tok{i}", [P, HG, P], F32) for i in range(2)]
        state = s.sb("state", [P, HG, NE, 32], F32)
        outT = s.sb("outT", [P, G4, P], F32)
        den = s.sb("den", [P, H], F32)
        o = s.sb("o", [P, H, DH], F32)
        oT = s.sb("oT", [P, DC, P], F32)
        y = s.sb("y", [P, D], F32)
        zeros = s.sb("zeros", [P, 2 * NE * 32], BF16)
        ps_a = [s.ps(f"ps_a{i}", [P, NE, P]) for i in range(HG)]
        ps_out = s.ps("ps_out", [P, G4, P])
        ps_s = s.ps("ps_s", [P, HG, NE, 32])
        ps_tok = s.ps("ps_tok", [P, H, 32])
        ps_o = ps_tok[:, 0:DC * P // 32].rearrange("p (k n) e -> p k (n e)", k=DC)
        ps_x = s.ps("ps_x", [P, 2, D])
        names = ("w_in", "ready", "copied", "q_ok", "a_ok", "masked_ok", "k_turned", "k_ok", "out_ok", "outT_ok",
                 "state_in", "state_ok", "turned", "den_ok", "o_ok", "o_turned", "oT_ok", "y_ok", "y_sum", "y_done",
                 "x_ok")
        (w_in, ready, copied, q_ok, a_ok, masked_ok, k_turned, k_ok, out_ok, outT_ok, state_in, state_ok, turned,
         den_ok, o_ok, o_turned, oT_ok, y_ok, y_sum, y_done, x_ok) = (s.sem(n) for n in names)
        block = s.engines()

        def run(engine, first, step):
            for b in range(B):
                c0 = b * CHUNKS
                first(b)

                def at_chunk(c):
                    step(b, *(c0 + n if 0 <= n < CHUNKS else None for n in range(c - 1, c + 3)), c % 2)

                for c in (-2, -1, 0):
                    at_chunk(c)
                with engine.Fori(0, CHUNKS // 2 - 2) as i:
                    for n in (1, 2):
                        c = 2 * i + (c0 + n)
                        step(b, c - 1, c, c + 1, c + 2, n % 2)
                for c in range(CHUNKS - 3, CHUNKS + 1):
                    at_chunk(c)

        @block.sync
        def _(sp):
            sp.dma_start(w[:], wo.rearrange("(k p) n -> p k n", p=P)).then_inc(w_in, 16)
            sp.dma_start(bias[:], bo.partition_broadcast(P)).then_inc(w_in, 16)
            sp.wait_ge(w_in, 32)

        @block.gpsimd
        def _(pool):
            pool.sem_inc(x_ok, 1)
            pool.wait_ge(ready, 1)

            def step(b, old, now, new, newer, at):
                if new is not None:
                    other = 1 - at
                    wait_apart(pool, state_in, new + 1, core.passed)
                    pool.tensor_copy(kc[other][:], kT[:, :, ds(new * P, P)])
                    pool.tensor_copy(vp[other][:, :, 0:DH].rearrange("p (a h) e -> p a h e", a=1),
                                     v[:, ds(new, 1), :].rearrange("p a (h e) -> p a h e", h=H)).then_inc(copied, 1)
                if old is not None:
                    wait_apart(pool, y_done, old + 1, core.passed)
                    pool.tensor_tensor(core.x[:, ds(old, 1), :], core.x[:, ds(old, 1), :],
                                       y[:].unsqueeze(1), ALU.add).then_inc(x_ok, 1)

            run(pool, lambda b: None, step)

        @block.scalar
        def _(act):
            def step(b, old, now, new, newer, at):
                if now is not None:
                    act.wait_ge(turned, now + 1)
                    act.wait_ge(out_ok, now + 1)
                    act.activation(outT[:], ps_out[:], ACT.Copy).then_inc(outT_ok, 1)
                if old is not None:
                    act.wait_ge(y_ok, old + 1)
                    act.wait_ge(o_turned, old + 1)
                    act.activation(oT[:], ps_o, ACT.Copy).then_inc(oT_ok, 1)
                if new is not None:
                    act.wait_ge(k_turned, new + 1)
                    act.activation(k_tok[1 - at][:], ps_x[:, 0].rearrange("p (g t) -> p g t", g=HG), ACT.Copy)\
                        .then_inc(k_ok, 1)

            run(act, lambda b: None, step)

        @block.vector
        def _(dve):
            for i in range(2):
                dve.memset(vp[i][:, :, DH:DH + 1], 1.0)
                dve.memset(vp[i][:, :, DH + 1:], 0.0)
            dve.memset(zeros[:], 0.0).then_inc(ready, 1)
            dve.wait_ge(w_in, 32)

            def first(b):
                if b > 0:
                    dve.wait_ge(out_ok, b * CHUNKS)
                dve.memset(state[:], 0.0).then_inc(state_ok, 1)

            def step(b, old, now, new, newer, at):
                def mask(hg):
                    dve.wait_ge(a_ok, new * HG + hg + 1)
                    dve.tensor_tensor(masked[1 - at][:, hg], ps_a[hg][:],
                                      core.c("upto").unsqueeze(1).broadcast_to([P, NE, P]), ALU.mult)\
                        .then_inc(masked_ok, 1)

                if now is not None:
                    dve.wait_ge(state_in, now + 3)
                    dve.tensor_tensor(state[:], ps_s[:], core.c("headof").unsqueeze(1).unsqueeze(3)
                                      .broadcast_to([P, HG, NE, 32]), ALU.mult).then_inc(state_ok, 1)
                if new is not None:
                    mask(0)
                if old is not None:
                    dve.wait_ge(y_ok, old + 2)
                    dve.wait_ge(x_ok, old + 1)
                    dve.tensor_tensor(y[:], ps_x[:, 1], bias[:], ALU.add).then_inc(y_sum, 1)
                    dve.wait_ge(y_sum, old + 1)
                    dve.tensor_tensor(y[:], y[:], core.rows[:, 1, b, GATE_A], ALU.mult).then_inc(y_done, 1)
                if new is not None:
                    mask(1)
                if now is not None:
                    dve.wait_ge(turned, now + 2)
                    dve.tensor_scalar(den[:], ps_tok[:, :, DH], DEN_EPS, None, ALU.add).then_inc(den_ok, 1)
                    dve.wait_ge(den_ok, now * 2 + 1)
                    dve.reciprocal(den[:], den[:]).then_inc(den_ok, 1)
                    dve.wait_ge(den_ok, now * 2 + 2)
                    dve.tensor_tensor(o[:], ps_tok[:, :, 0:DH], den[:].unsqueeze(2).broadcast_to([P, H, DH]),
                                      ALU.mult).then_inc(o_ok, 1)
                if newer is not None:
                    for hg in range(HG):
                        dve.tensor_tensor(qblk[:, hg], qT[:, hg:hg + 1, ds(newer * P, P)].broadcast_to([P, NE, P]),
                                          core.c("headof").unsqueeze(2).broadcast_to([P, NE, P]), ALU.mult)\
                            .then_inc(q_ok, 1)

            run(dve, first, step)

        @block.tensor
        def _(pe):
            pe.sem_inc(state_in, 2)
            pe.sem_inc(turned, 1)
            pe.sem_inc(y_ok, 1)
            pe.wait_ge(ready, 1)
            pe.wait_ge(w_in, 32)

            def first(b):
                pe.wait_ge(state_ok, b * CHUNKS + b + 1)
                pe.matmul(ps_s[:].rearrange("p g h e -> p (g h e)"), core.ident_bf[:], zeros[:], start=True,
                          stop=False, skip_group_check=True)

            def step(b, old, now, new, newer, at):
                def products(hg):
                    pe.wait_ge(q_ok, new * HG + hg + 1)
                    for n in range(2):
                        last = pe.matmul(ps_a[hg][:, 4 * n:4 * n + 4].rearrange("p h t -> p (h t)"),
                                         kc[1 - at][:, hg],
                                         qblk[:, hg, 4 * n:4 * n + 4].rearrange("p h t -> p (h t)"),
                                         start=True, stop=True)
                    last.then_inc(a_ok, 1)

                if now is not None:
                    pe.wait_ge(masked_ok, (now + 1) * HG)
                    pe.wait_ge(state_ok, now + (b + 1))
                    for g4 in range(G4):
                        hg, half = g4 // 2, g4 % 2
                        pe.matmul(ps_out[:, g4:g4 + 1], state[:, hg, 4 * half:4 * half + 4].rearrange("p h e -> p (h e)"),
                                  qT[:, hg:hg + 1, ds(now * P, P)], start=True, stop=False, skip_group_check=True)
                        for n in range(4):
                            h = 4 * g4 + n
                            last = pe.matmul(ps_out[32 * n:32 * n + 32, g4], vp[at][:, h], masked[at][:, hg, h % NE],
                                             start=False, stop=(n == 3), tile_position=(0, 32 * n),
                                             skip_group_check=True)
                    last.then_inc(out_ok, 1)
                    pe.wait_ge(k_ok, now + 1)
                    for hg in range(HG):
                        last = pe.matmul(ps_s[:, hg].rearrange("p h e -> p (h e)"), k_tok[at][:, hg],
                                         vp[at][:, hg * NE:(hg + 1) * NE].rearrange("p h e -> p (h e)"),
                                         start=False, stop=False, skip_group_check=True)
                    last.then_inc(state_in, 1)
                if old is not None:
                    pe.wait_ge(o_ok, old + 1)
                    for k in range(DC):
                        last = pe.transpose(ps_o[:, k], o[:, 8 * k:8 * k + 8].rearrange("p h e -> p (h e)"),
                                            core.c("ident"))
                    last.then_inc(o_turned, 1)
                if new is not None:
                    pe.wait_ge(copied, new + 1)
                    products(0)
                if old is not None:
                    pe.wait_ge(oT_ok, old + 1)
                    for k in range(DC):
                        last = pe.matmul(ps_x[:, 1], oT[:, k], w[:, k], start=(k == 0), stop=(k == DC - 1))
                    last.then_inc(y_ok, 1)
                if new is not None:
                    products(1)
                    if old is not None:
                        pe.wait_ge(y_sum, old + 1)
                    for hg in range(HG):
                        last = pe.transpose(ps_x[:, 0, hg * P:(hg + 1) * P], kc[1 - at][:, hg], core.c("ident"))
                    last.then_inc(k_turned, 1)
                if now is not None:
                    pe.wait_ge(outT_ok, now + 1)
                    for g4 in range(G4):
                        last = pe.transpose(ps_tok[:, 4 * g4:4 * g4 + 4].rearrange("p h e -> p (h e)"), outT[:, g4],
                                            core.c("ident"))
                    last.then_inc(turned, 1)

            run(pe, first, step)


def route1(nc, core, scores, source, weight):
    with stage(nc, "route1") as s:
        most = s.sb("most", [P, T], F32)
        other = s.sb("other", [P, T, NE], F32)
        mask = s.sb("mask", [P, T, NE], F32)
        sums = [s.sb(f"sums{i}", [P, T, NE], F32) for i in range(2)]
        row = s.sb("row", [P, T], F32)
        place = s.sb("place", [P, T, NE], F32)
        ps_in = s.ps("ps_in", [P, T, NE])
        ps_all = s.ps("ps_all", [P, T, NE])
        steps, mask_ok, sums_ok = (s.sem(n) for n in ("steps", "mask_ok", "sums_ok"))
        block = s.engines()
        wide = most[:].unsqueeze(2).broadcast_to([P, T, NE])
        experts = core.c("expert").unsqueeze(1).broadcast_to([P, T, NE])
        bases = core.c("expert_base").unsqueeze(1).broadcast_to([P, T, NE])

        @block.vector
        def _(dve):
            link = Counted(dve, steps).then
            link(dve.tensor_reduce(most[:], scores[:], AX.X, ALU.max))
            link(dve.tensor_tensor(other[:], scores[:], wide, ALU.is_lt))
            link(dve.tensor_scalar(other[:], other[:], 100.0, None, ALU.mult))
            link(dve.tensor_tensor(other[:], other[:], experts, ALU.add))
            link(dve.tensor_reduce(most[:], other[:], AX.X, ALU.min))
            dve.tensor_tensor(mask[:], wide, experts, ALU.is_equal).then_inc(mask_ok, 1)
            chain = Counted(dve, steps, 5)
            prefix(dve, (sums_ok, 1), chain, mask, ps_in, ps_all, sums, place)
            link = chain.then
            link(dve.tensor_scalar(other[:], place[:], float(CAP1), None, ALU.is_lt))
            link(dve.tensor_tensor(mask[:], mask[:], other[:], ALU.mult))
            link(dve.tensor_tensor(other[:], mask[:], scores[:], ALU.mult))
            link(dve.tensor_reduce(weight[:], other[:], AX.X, ALU.add))
            link(dve.tensor_tensor(other[:], place[:], bases, ALU.add))
            link(dve.tensor_scalar(other[:], other[:], float(-S), None, ALU.add))
            link(dve.tensor_tensor(other[:], other[:], mask[:], ALU.mult))
            link(dve.tensor_reduce(row[:], other[:], AX.X, ALU.add))
            link(dve.tensor_scalar(source[:], row[:], float(S), None, ALU.add))

        @block.tensor
        def _(pe):
            flat = mask[:].rearrange("p t e -> p (t e)")
            pe.wait_ge(mask_ok, 1)
            pe.matmul(ps_in[:].rearrange("p t e -> p (t e)"), core.c("before"), flat, start=True, stop=True)
            pe.matmul(ps_all[:].rearrange("p t e -> p (t e)"), core.c("ones"), flat, start=True, stop=True)\
                .then_inc(sums_ok, 1)


def listing1(nc, core, source, slots):
    COLS = NE * CAP1 // P
    PART = T // 4
    with stage(nc, "list1") as s:
        low_i = s.sb("low_i", [P, T], I32)
        high_i = s.sb("high_i", [P, T], I32)
        low = s.sb("low", [P, T], BF16)
        high = s.sb("high", [P, T], F32)
        iota = s.sb("iota", [P, P], BF16)
        hot = s.sb("hot", [P, T, COLS], F32)
        marks = s.sb("marks", [P, T, 2, COLS], BF16)
        hot_low = s.sb("hot_low", [P, T, P], BF16)
        tokens = s.sb("tokens", [P, COLS], F32)
        ps = s.ps("ps_list", [P, 2, COLS])
        steps, marks_ok, low_ok, done = (s.sem(n) for n in ("steps", "marks_ok", "low_ok", "done"))
        block = s.engines()

        @block.vector
        def _(dve):
            chain = Counted(dve, steps)
            dve.tensor_single_scalar(low_i[:], source[:], P - 1, ALU.bitwise_and)
            dve.tensor_single_scalar(high_i[:], source[:], 7, ALU.arith_shift_right)
            chain.then(dve.tensor_copy(iota[:], core.c("iota")))
            dve.tensor_copy(low[:], low_i[:])
            chain.then(dve.tensor_copy(high[:], high_i[:]))
            chain.then(dve.tensor_tensor(hot[:], high[:].unsqueeze(2).broadcast_to([P, T, COLS]),
                                         core.c("iota")[:, 0:COLS].unsqueeze(1).broadcast_to([P, T, COLS]),
                                         ALU.is_equal))
            dve.tensor_scalar(marks[:, :, 0], hot[:], core.c("part"), None, ALU.mult)
            tiles = core.c("tile_of").rearrange("p (t e) -> p t e", e=NE)[:, :, 0:1]
            dve.tensor_tensor(marks[:, :, 1], hot[:], tiles.broadcast_to([P, T, COLS]), ALU.mult)\
                .then_inc(marks_ok, 1)
            for n in range(T // PART):
                part = slice(n * PART, (n + 1) * PART)
                dve.tensor_tensor(hot_low[:, part], low[:, part].unsqueeze(2).broadcast_to([P, PART, P]),
                                  iota[:].unsqueeze(1).broadcast_to([P, PART, P]), ALU.is_equal).then_inc(low_ok, 1)
            dve.wait_ge(done, 1)
            chain.then(dve.tensor_scalar(tokens[:], ps[:, 1], float(P), None, ALU.mult))
            chain.then(dve.tensor_tensor(slots[:], tokens[:], ps[:, 0], ALU.add))

        @block.tensor
        def _(pe):
            pe.wait_ge(marks_ok, 1)
            for t in range(T):
                if t % PART == 0:
                    pe.wait_ge(low_ok, t // PART + 1)
                last = pe.matmul(ps[:].rearrange("p w c -> p (w c)"), hot_low[:, t],
                                 marks[:, t].rearrange("p w c -> p (w c)"), start=(t == 0), stop=(t == T - 1))
            last.then_inc(done, 1)


def experts1(nc, core, h_rows, slots, w1, w2, outputs):
    CH = CAP1 // P
    MC = HID1 // P
    RING = 4
    with stage(nc, "experts1") as s:
        w_up = [s.sb(f"w1_{i}", [P, DC, HID1], F32) for i in range(2)]
        w_down = [s.sb(f"w2_{i}", [P, MC, D], F32) for i in range(2)]
        index = [s.sb(f"index{i}", [P, CH], I32) for i in range(2)]
        rows = [s.sb(f"gathered{i}", [P, CH, D], F32) for i in range(2)]
        xT = [s.sb(f"xT{i}", [P, DC, GROUP], F32) for i in range(2)]
        hT = s.sb("hidT", [P, MC, GROUP], F32)
        out = [s.sb(f"out{i}", [P, CH, D], F32) for i in range(2)]
        zeros = s.sb("zeros", [1, D], F32)
        ps_t = s.ps("ps_t", [P, DC, GROUP])
        ps_a = [s.ps(f"ps_a{i}", [P, GROUP]) for i in range(RING)]
        ps_y = [s.ps(f"ps_y{i}", [P, 2, D]) for i in range(2)]
        names = ("zero_ok", "zero_out", "index_ok", "turned", "xT_ok", "up_ok", "hid_ok", "relu_ok", "down_ok",
                 "out_ok")
        (zero_ok, zero_out, index_ok, turned, xT_ok, up_ok, hid_ok, relu_ok, down_ok, out_ok) = (
            s.sem(n) for n in names)
        w_in = [s.sem(f"w_in{i}") for i in range(2)]
        gathered = [s.sem(f"gathered{i}") for i in range(2)]
        stored = [s.sem(f"stored{i}") for i in range(2)]
        block = s.engines()

        @block.sync
        def _(sp):
            def load(e, at):
                for to, w in ((w_up, w1), (w_down, w2)):
                    sp.dma_start(to[at][:], w[ds(e, 1)].rearrange("e (k p) n -> p (e k) n", p=P)).then_inc(
                        w_in[at], 16)

            load(0, 0)
            load(1, 1)
            for at in range(2):
                sp.sem_inc(stored[at], 16)
            sp.wait_ge(zero_ok, 1)
            sp.dma_start(outputs[S:S + 1, :], zeros[:]).then_inc(zero_out, 16)
            sp.wait_ge(zero_out, 16)

            def store(e, at):
                start = e * CAP1 if isinstance(e, int) else sp.snap(e * CAP1)
                wait_apart(sp, out_ok, e * 2 + 4, core.passed)
                sp.dma_start(outputs[ds(start, CAP1)].rearrange("(c p) d -> p c d", p=P), out[at][:]).then_inc(
                    stored[at], 16)

            with sp.Fori(0, NE // 2 - 1) as i:
                for at in range(2):
                    e = sp.snap(2 * i + (at + 2))
                    store(2 * i + at, at)
                    load(e, at)
            for at in range(2):
                store(NE - 2 + at, at)
            for at in range(2):
                sp.wait_ge(stored[at], (NE // 2 + 1) * 16)

        @block.gpsimd
        def _(pool):
            pool.memset(zeros[:], 0.0).then_inc(zero_ok, 1)

            def step(now, after):
                if after is not None:
                    wait_apart(pool, turned, after.u + 1, core.passed)
                    pool.tensor_copy(index[after.at][:], slots[:, ds(after.e * CH, CH)]).then_inc(index_ok, 1)
                    wait_apart(pool, index_ok, after.e + 1, core.passed)
                    for c in range(CH):
                        pool.indirect_dma_start(
                            rows[after.at][:, c], None, h_rows,
                            bass.IndirectOffsetOnAxis(ap=index[after.at][:, c:c + 1], axis=0))\
                            .then_inc(gathered[after.at], 16)

            unit_steps(pool, 1, step)

        @block.scalar
        def _(act):
            act.sem_inc(out_ok, 2)

            def step(now, after):
                if now is not None:
                    for m in range(0, MC, 2):
                        act.wait_ge(up_ok, now.u * MC + m + 1)
                        act.activation(hT[:, m], ps_a[m % RING][:], ACT.Relu).then_inc(hid_ok, 1)
                if after is not None:
                    act.wait_ge(turned, after.u + 3)
                    act.activation(xT[after.at][:], ps_t[:], ACT.Copy).then_inc(xT_ok, 1)
                if now is not None:
                    act.wait_ge(stored[now.at], now.pair * 16 + 16)
                    for n in range(2):
                        act.wait_ge(down_ok, now.u * 2 + n + 1)
                        act.activation(out[now.at][:, 2 * n:2 * n + 2], ps_y[n][:], ACT.Copy).then_inc(out_ok, 1)

            unit_steps(act, 1, step)

        @block.vector
        def _(dve):
            def step(now, after):
                if now is not None:
                    for m in range(1, MC, 2):
                        dve.wait_ge(up_ok, now.u * MC + m + 1)
                        dve.tensor_scalar(hT[:, m], ps_a[m % RING][:], 0.0, None, ALU.max).then_inc(relu_ok, 1)

            unit_steps(dve, 1, step)

        @block.tensor
        def _(pe):
            pe.sem_inc(turned, 2)

            def step(now, after):
                if now is not None:
                    pe.wait_ge(xT_ok, now.u + 1)
                    wait_apart(pe, w_in[now.at], now.pair * 32 + 32, core.passed)
                    for m in range(MC):
                        if m >= RING:
                            pe.wait_ge((hid_ok, relu_ok)[m % 2], now.u * (MC // 2) + (m - RING) // 2 + 1)
                        for k in range(DC):
                            last = pe.matmul(ps_a[m % RING][:], w_up[now.at][:, k, m * P:(m + 1) * P],
                                             xT[now.at][:, k], start=(k == 0), stop=(k == DC - 1))
                        last.then_inc(up_ok, 1)
                if after is not None:
                    wait_apart(pe, gathered[after.at], after.pair * (CH * 16) + CH * 16, core.passed)
                    for k in range(DC):
                        for j in range(CH):
                            last = pe.transpose(ps_t[:, k, j * P:(j + 1) * P], rows[after.at][:, j, k * P:(k + 1) * P],
                                                core.c("ident"))
                    last.then_inc(turned, 1)
                if now is not None:
                    pe.wait_ge(hid_ok, (now.u + 1) * (MC // 2))
                    pe.wait_ge(relu_ok, (now.u + 1) * (MC // 2))
                    for n in range(2):
                        pe.wait_ge(out_ok, now.u * 2 + n + 1)
                        for c in range(2):
                            for m in range(MC):
                                last = pe.matmul(ps_y[n][:, c], hT[:, m, (2 * n + c) * P:(2 * n + c + 1) * P],
                                                 w_down[now.at][:, m], start=(m == 0), stop=(m == MC - 1))
                        last.then_inc(down_ok, 1)

            unit_steps(pe, 1, step)


def finish(nc, core, outputs, source, weight, result):
    HALF = 4
    RING = 2 * HALF
    with stage(nc, "finish") as s:
        index = [s.sb(f"index{i}", [P, HALF], I32) for i in range(2)]
        rows = [s.sb(f"rows{i}", [P, 1, D], F32) for i in range(RING)]
        gated = s.sb("gated", [P, RING, 1, D], F32)
        index_ok, gated_ok, x_ok, out = (s.sem(n) for n in ("index_ok", "gated_ok", "x_ok", "out"))
        gathered = [s.sem(f"gathered{i}") for i in range(RING)]
        block = s.engines()
        PAIRS = T // B // RING

        def run(engine, step):
            for b in range(B):
                with engine.Fori(b * PAIRS, (b + 1) * PAIRS) as i:
                    step(b, i)

        @block.gpsimd
        def _(pool):
            def step(b, i):
                for half in range(2):
                    wait_apart(pool, gated_ok, i * RING + (half + 1) * HALF, core.passed)
                    pool.tensor_copy(index[half][:], source[:, ds(i * RING + half * HALF, HALF)]).then_inc(index_ok, 1)
                    wait_apart(pool, index_ok, i * 2 + (half + 1), core.passed)
                    for n in range(HALF):
                        pool.indirect_dma_start(rows[half * HALF + n][:, 0], None, outputs,
                                                bass.IndirectOffsetOnAxis(ap=index[half][:, n:n + 1], axis=0))\
                            .then_inc(gathered[half * HALF + n], 16)

            run(pool, step)

        @block.vector
        def _(dve):
            dve.sem_inc(gated_ok, RING)

            def step(b, i):
                for n in range(RING):
                    t = i * RING + n
                    dve.wait_ge(gathered[n], i * 16 + 16)
                    dve.scalar_tensor_tensor(gated[:, n], rows[n][:], weight[:, ds(t, 1)],
                                             core.rows[:, 1, b, GATE_B:GATE_B + 1], ALU.mult, ALU.mult)\
                        .then_inc(gated_ok, 1)
                    dve.wait_ge(gated_ok, t + 1 + RING)
                    dve.tensor_tensor(core.x[:, ds(t, 1), :], core.x[:, ds(t, 1), :], gated[:, n], ALU.add)\
                        .then_inc(x_ok, 1)

            run(dve, step)

        @block.sync
        def _(sp):
            view = result.rearrange("b (t p) d -> p (b t) d", p=P)

            def step(b, i):
                for half in range(2):
                    tile = sp.snap(i * RING + half * HALF)
                    wait_apart(sp, x_ok, i * RING + (half + 1) * HALF, core.passed)
                    sp.dma_start(view[:, ds(tile, HALF)], core.x[:, ds(tile, HALF)]).then_inc(out, 16)

            run(sp, step)
            sp.wait_ge(out, B * PAIRS * 2 * 16)


def program(nc, X, consts, cT0, wmod0, cT1, wmod1, wq0, wk0, wv0, wo0, lq1, lk1, lq2, lk2, rms_scale, wg0, e_w1,
            e_w3, e_w2, wq1, bq1, wk1, bk1, wv1, bv1, wo1, bo1, wg1, f_w1, f_w2, result):
    qk_parts = nc.dram_tensor("qk_parts", (3, 2, HEADS, DV, N), BF16, kind="Internal").ap()
    oT = nc.dram_tensor("heads_out", (HEADS, 2 * DV, N), F32, kind="Internal").ap()
    sums = nc.dram_tensor("exp_sums", (HEADS, 4, N), F32, kind="Internal").ap()
    h0_rows = nc.dram_tensor("h0_rows", (S, D + NE), F32, kind="Internal").ap()
    added = nc.dram_tensor("experts0_sum", (S, D), F32, kind="Internal").ap()
    h1_rows = nc.dram_tensor("h1_rows", (S, D), F32, kind="Internal").ap()
    outputs = nc.dram_tensor("experts1_out", (S + 1, D), F32, kind="Internal").ap()
    with ExitStack() as ctx:
        core = Core(nc, ctx)
        setup(nc, core, X, consts, (cT0, cT1), (wmod0, wmod1))
        with stage(nc, "heads") as s:
            v = s.sb("v", [P, HEADS, K_TILES, DV], F32)
            project0(nc, core, (wq0, wk0, wv0), qk_parts, v)
            attention0(nc, core, qk_parts, v, oT, sums)
        attention0_out(nc, core, oT, sums, (lq1, lk1, lq2, lk2), rms_scale, wo0)
        scores = core.sb("scores", [P, T, NE], F32)
        place = core.sb("place", [P, T, NE], F32)
        slots0 = core.sb("slots0", [P, NE, CAP0 // P], I32)
        slots1 = core.sb("slots1", [P, NE * CAP1 // P], I32)
        gates(nc, core, 0, wg0, h0_rows, scores)
        route0(nc, core, scores, place)
        listing0(nc, core, place, slots0)
        experts0(nc, core, h0_rows, slots0[:].rearrange("p e c -> p (e c)"), e_w1, e_w3, e_w2, added)
        with stage(nc, "linear") as s:
            qT = s.sb("qT", [P, DC, S], F32)
            kT = s.sb("kT", [P, DC, S], F32)
            v = s.sb("v", [P, T, D], F32)
            project1(nc, core, added, wq1, wk1, wv1, bq1, bk1, bv1, qT, kT, v)
            linear1(nc, core, wo1, bo1, qT, kT, v)
        gates(nc, core, 1, wg1, h1_rows, scores)
        source = core.sb("source", [P, T], I32)
        weight = core.sb("weight", [P, T], F32)
        route1(nc, core, scores, source, weight)
        listing1(nc, core, source, slots1)
        experts1(nc, core, h1_rows, slots1, f_w1, f_w2, outputs)
        finish(nc, core, outputs, source, weight, result)


def kernel(**inputs):
    import numpy as np
    from concourse import bacc
    from concourse.bass_utils import run_bass_kernel_spmd

    def turned(name):
        return np.ascontiguousarray(np.asarray(inputs[name]).T)

    def interleaved(name):
        w = turned(name)
        return np.ascontiguousarray(w.reshape(D, H, 2, DH).transpose(0, 1, 3, 2).reshape(D, DQ))

    def plain(name):
        return np.ascontiguousarray(np.asarray(inputs[name]))

    arrays = {
        "X": plain("L0_attn_X"), "consts": constants(np),
        "cT0": turned("L0_c"), "wmod0": plain("L0_wmod"), "cT1": turned("L1_c"), "wmod1": plain("L1_wmod"),
        "wq0": interleaved("L0_attn_W_q"), "wk0": interleaved("L0_attn_W_k"), "wv0": turned("L0_attn_W_v"),
        "wo0": turned("L0_attn_W_o"), "lq1": plain("L0_attn_lambda_q1"), "lk1": plain("L0_attn_lambda_k1"),
        "lq2": plain("L0_attn_lambda_q2"), "lk2": plain("L0_attn_lambda_k2"),
        "rms_scale": plain("L0_attn_rms_scale"), "wg0": plain("L0_ffn_wg"), "e_w1": plain("L0_ffn_w1"),
        "e_w3": plain("L0_ffn_w3"), "e_w2": plain("L0_ffn_w2"), "wq1": plain("L1_attn_wq"),
        "bq1": plain("L1_attn_bq"), "wk1": plain("L1_attn_wk"), "bk1": plain("L1_attn_bk"),
        "wv1": plain("L1_attn_wv"), "bv1": plain("L1_attn_bv"), "wo1": plain("L1_attn_wo"),
        "bo1": plain("L1_attn_bo"), "wg1": plain("L1_ffn_wg"), "f_w1": plain("L1_ffn_w1"), "f_w2": plain("L1_ffn_w2"),
    }
    nc = bacc.Bacc("TRN2", target_bir_lowering=False, num_devices=1)
    given = {name: nc.dram_tensor(f"in_{name}", a.shape, mybir.dt.from_np(a.dtype), kind="ExternalInput").ap()
             for name, a in arrays.items()}
    result = nc.dram_tensor("result", (B, N, D), F32, kind="ExternalOutput").ap()
    program(nc, **given, result=result)
    done = run_bass_kernel_spmd(nc, [{f"in_{name}": a for name, a in arrays.items()}], core_ids=[0])
    return done.results[0]["result"]
```
